# Optimizing a Trainium2 kernel written in Bass

```python
import numpy as np
import jax
import jax.numpy as jnp

def _softmax(x, axis=-1):
    return jax.nn.softmax(x, axis=axis)
def _gelu(x):
    return jax.nn.gelu(x, approximate=True)
def _silu(x):
    return jax.nn.silu(x)
def _sigmoid(x):
    return jax.nn.sigmoid(x)
def _layernorm(x, axis=-1, eps=1e-5):
    m = jnp.mean(x, axis=axis, keepdims=True)
    v = jnp.var(x, axis=axis, keepdims=True)
    return (x - m) / jnp.sqrt(v + eps)
def _scatter_add(tgt, idx, src, axis=0):
    return tgt.at[idx].add(src)
def _segment_sum(src, seg, n):
    return jax.ops.segment_sum(src, seg, n)

kernel_name = 'mk_conv_preact_d2_conv_nchw256_f65ef7'

def setup_inputs(seed: int = 0):
    np.random.seed(seed)
    _w = jnp.asarray
    def _rec_inputs():
        import jax
        import jax.numpy as jnp
        _gk = jax.random.key(seed)
        x = -0.0005207 + 1.001 * jax.random.normal(jax.random.fold_in(_gk, 1), (2, 256, 64, 64), jnp.float32)
        return x
    x = _rec_inputs()
    def _L0_conv_setup():
        import jax, jax.numpy as jnp
        import numpy as np
        B, C, H, W = (2, 256, 64, 64)
        NUM_HEADS = 4
        DIM_HEAD_QK = 64
        DIM_HEAD_V = 64
        DIM_OUT_QK = NUM_HEADS * DIM_HEAD_QK
        DIM_OUT_V = NUM_HEADS * DIM_HEAD_V
        SCALE = DIM_HEAD_QK ** (-0.5)

        def rel_logits_1d(q, rel_k, permute):
            Bh, Hq, Wq, d = q.shape
            R = 2 * Wq - 1
            x = jnp.einsum('bhwd,rd->bhwr', q, rel_k)
            x = x.reshape(-1, Wq, R)
            x_pad = jnp.pad(x, ((0, 0), (0, 0), (0, 1))).reshape(x.shape[0], -1)
            x_pad = jnp.pad(x_pad, ((0, 0), (0, Wq - 1)))
            x_pad = x_pad.reshape(-1, Wq + 1, R)
            x = x_pad[:, :Wq, Wq - 1:]
            x = x.reshape(Bh, Hq, 1, Wq, Wq)
            x = jnp.broadcast_to(x, (Bh, Hq, Hq, Wq, Wq))
            return jnp.transpose(x, permute)

        def pos_embed_rel(q, height_rel, width_rel):
            Bh = q.shape[0]
            qr = q.reshape(Bh, H, W, -1)
            rel_w = rel_logits_1d(qr, width_rel, (0, 1, 3, 2, 4))
            qt = jnp.transpose(qr, (0, 2, 1, 3))
            rel_h = rel_logits_1d(qt, height_rel, (0, 3, 1, 4, 2))
            return (rel_h + rel_w).reshape(Bh, H * W, H * W)
        key = jax.random.key(seed)
        k1, k2, k3, k4 = jax.random.split(key, 4)
        x = jax.random.normal(k1, (B, C, H, W), dtype=jnp.float32)
        qkv_w = jax.random.normal(k2, (2 * DIM_OUT_QK + DIM_OUT_V, C), dtype=jnp.float32) * C ** (-0.5)
        height_rel = jax.random.normal(k3, (2 * H - 1, DIM_HEAD_QK), dtype=jnp.float32) * SCALE
        width_rel = jax.random.normal(k4, (2 * W - 1, DIM_HEAD_QK), dtype=jnp.float32) * SCALE
        return {'x': x, 'qkv_w': qkv_w, 'height_rel': height_rel, 'width_rel': width_rel}
    _L0_conv_all = _L0_conv_setup()
    _L0_conv_in = {k: v for k, v in _L0_conv_all.items() if k in ('qkv_w', 'height_rel', 'width_rel', )}
    del _L0_conv_all

    def _L1_conv_setup():
        import jax, jax.numpy as jnp
        import numpy as np
        DIM, D_STATE, D_CONV, D_INNER, DT_RANK = (256, 16, 4, 512, 16)

        def _mamba_forward(seq, in_proj_w, conv_w, conv_b, x_proj_w, dt_proj_w, dt_proj_b, A_log, D):
            Bsz, L, _ = seq.shape
            xz = seq @ in_proj_w.T
            u, z = jnp.split(xz, 2, axis=-1)
            up = jnp.pad(u, ((0, 0), (D_CONV - 1, 0), (0, 0)))
            u = sum((up[:, k:k + L, :] * conv_w[:, k] for k in range(D_CONV))) + conv_b
            u = jax.nn.silu(u)
            xdbc = u @ x_proj_w.T
            dt = xdbc[..., :DT_RANK]
            Bmat = xdbc[..., DT_RANK:DT_RANK + D_STATE]
            Cmat = xdbc[..., DT_RANK + D_STATE:]
            delta = jax.nn.softplus(dt @ dt_proj_w.T + dt_proj_b)
            A = -jnp.exp(A_log)

            def step(h, ins):
                d_t, B_t, C_t, u_t = ins
                dA = jnp.exp(d_t[:, :, None] * A)
                h = dA * h + (d_t * u_t)[:, :, None] * B_t[:, None, :]
                y = jnp.einsum('bdn,bn->bd', h, C_t)
                return (h, y)
            h0 = jnp.zeros((Bsz, D_INNER, D_STATE), seq.dtype)
            xs = (delta.transpose(1, 0, 2), Bmat.transpose(1, 0, 2), Cmat.transpose(1, 0, 2), u.transpose(1, 0, 2))
            _, ys = jax.lax.scan(step, h0, xs)
            y = ys.transpose(1, 0, 2)
            y = y + u * D
            y = y * jax.nn.silu(z)
            return y
        key = jax.random.key(seed)
        ks = jax.random.split(key, 12)
        s = 0.02
        B, H, W = (8, 64, 64)
        inp = {'x_feat': jax.random.normal(ks[0], (B, DIM, H, W), jnp.float32), 'to_seq_w': jax.random.normal(ks[1], (DIM, DIM), jnp.float32) * s, 'to_seq_b': jnp.zeros((DIM,), jnp.float32), 'in_proj_w': jax.random.normal(ks[2], (2 * D_INNER, DIM), jnp.float32) * s, 'conv_w': jax.random.normal(ks[3], (D_INNER, D_CONV), jnp.float32) * s, 'conv_b': jnp.zeros((D_INNER,), jnp.float32), 'x_proj_w': jax.random.normal(ks[4], (DT_RANK + 2 * D_STATE, D_INNER), jnp.float32) * s, 'dt_proj_w': jax.random.normal(ks[5], (D_INNER, DT_RANK), jnp.float32) * s, 'dt_proj_b': jax.random.uniform(ks[6], (D_INNER,), jnp.float32, -4.0, -2.0), 'A_log': jnp.log(jnp.broadcast_to(jnp.arange(1, D_STATE + 1, dtype=jnp.float32), (D_INNER, D_STATE))), 'D': jnp.ones((D_INNER,), jnp.float32), 'out_proj_w': jax.random.normal(ks[7], (DIM, D_INNER), jnp.float32) * s, 'from_seq_w': jax.random.normal(ks[8], (DIM, DIM), jnp.float32) * s, 'from_seq_b': jnp.zeros((DIM,), jnp.float32)}
        return inp
    _L1_conv_all = _L1_conv_setup()
    _L1_conv_in = {k: v for k, v in _L1_conv_all.items() if k in ('to_seq_w', 'to_seq_b', 'in_proj_w', 'conv_w', 'conv_b', 'x_proj_w', 'dt_proj_w', 'dt_proj_b', 'A_log', 'D', 'out_proj_w', 'from_seq_w', 'from_seq_b', )}
    del _L1_conv_all

    return {
        "x": x,
        "L0_conv_qkv_w": _L0_conv_in["qkv_w"],
        "L0_conv_height_rel": _L0_conv_in["height_rel"],
        "L0_conv_width_rel": _L0_conv_in["width_rel"],
        "L1_conv_to_seq_w": _L1_conv_in["to_seq_w"],
        "L1_conv_to_seq_b": _L1_conv_in["to_seq_b"],
        "L1_conv_in_proj_w": _L1_conv_in["in_proj_w"],
        "L1_conv_conv_w": _L1_conv_in["conv_w"],
        "L1_conv_conv_b": _L1_conv_in["conv_b"],
        "L1_conv_x_proj_w": _L1_conv_in["x_proj_w"],
        "L1_conv_dt_proj_w": _L1_conv_in["dt_proj_w"],
        "L1_conv_dt_proj_b": _L1_conv_in["dt_proj_b"],
        "L1_conv_A_log": _L1_conv_in["A_log"],
        "L1_conv_D": _L1_conv_in["D"],
        "L1_conv_out_proj_w": _L1_conv_in["out_proj_w"],
        "L1_conv_from_seq_w": _L1_conv_in["from_seq_w"],
        "L1_conv_from_seq_b": _L1_conv_in["from_seq_b"],
    }

def reference(x, L0_conv_qkv_w, L0_conv_height_rel, L0_conv_width_rel, L1_conv_to_seq_w, L1_conv_to_seq_b, L1_conv_in_proj_w, L1_conv_conv_w, L1_conv_conv_b, L1_conv_x_proj_w, L1_conv_dt_proj_w, L1_conv_dt_proj_b, L1_conv_A_log, L1_conv_D, L1_conv_out_proj_w, L1_conv_from_seq_w, L1_conv_from_seq_b):
    import jax
    import jax.numpy as jnp
    def _L0_conv_ref(x, qkv_w, height_rel, width_rel):
        import jax, jax.numpy as jnp
        import numpy as np
        B, C, H, W = (2, 256, 64, 64)
        NUM_HEADS = 4
        DIM_HEAD_QK = 64
        DIM_HEAD_V = 64
        DIM_OUT_QK = NUM_HEADS * DIM_HEAD_QK
        DIM_OUT_V = NUM_HEADS * DIM_HEAD_V
        SCALE = DIM_HEAD_QK ** (-0.5)

        def rel_logits_1d(q, rel_k, permute):
            Bh, Hq, Wq, d = q.shape
            R = 2 * Wq - 1
            x = jnp.einsum('bhwd,rd->bhwr', q, rel_k)
            x = x.reshape(-1, Wq, R)
            x_pad = jnp.pad(x, ((0, 0), (0, 0), (0, 1))).reshape(x.shape[0], -1)
            x_pad = jnp.pad(x_pad, ((0, 0), (0, Wq - 1)))
            x_pad = x_pad.reshape(-1, Wq + 1, R)
            x = x_pad[:, :Wq, Wq - 1:]
            x = x.reshape(Bh, Hq, 1, Wq, Wq)
            x = jnp.broadcast_to(x, (Bh, Hq, Hq, Wq, Wq))
            return jnp.transpose(x, permute)

        def pos_embed_rel(q, height_rel, width_rel):
            Bh = q.shape[0]
            qr = q.reshape(Bh, H, W, -1)
            rel_w = rel_logits_1d(qr, width_rel, (0, 1, 3, 2, 4))
            qt = jnp.transpose(qr, (0, 2, 1, 3))
            rel_h = rel_logits_1d(qt, height_rel, (0, 3, 1, 4, 2))
            return (rel_h + rel_w).reshape(Bh, H * W, H * W)
        qkv = jnp.einsum('bchw,oc->bohw', x, qkv_w)
        q, k, v = jnp.split(qkv, [DIM_OUT_QK, 2 * DIM_OUT_QK], axis=1)
        HW = H * W
        q = q.reshape(B * NUM_HEADS, DIM_HEAD_QK, HW).transpose(0, 2, 1)
        k = k.reshape(B * NUM_HEADS, DIM_HEAD_QK, HW)
        v = v.reshape(B * NUM_HEADS, DIM_HEAD_V, HW).transpose(0, 2, 1)
        attn = jnp.einsum('bnd,bdm->bnm', q, k) * SCALE + pos_embed_rel(q, height_rel, width_rel)
        attn = jax.nn.softmax(attn, axis=-1)
        out = jnp.einsum('bnm,bmd->bnd', attn, v)
        out = out.transpose(0, 2, 1).reshape(B, DIM_OUT_V, H, W)
        return out

    def _L1_conv_ref(x_feat, to_seq_w, to_seq_b, in_proj_w, conv_w, conv_b, x_proj_w, dt_proj_w, dt_proj_b, A_log, D, out_proj_w, from_seq_w, from_seq_b):
        import jax, jax.numpy as jnp
        import numpy as np
        DIM, D_STATE, D_CONV, D_INNER, DT_RANK = (256, 16, 4, 512, 16)

        def _mamba_forward(seq, in_proj_w, conv_w, conv_b, x_proj_w, dt_proj_w, dt_proj_b, A_log, D):
            Bsz, L, _ = seq.shape
            xz = seq @ in_proj_w.T
            u, z = jnp.split(xz, 2, axis=-1)
            up = jnp.pad(u, ((0, 0), (D_CONV - 1, 0), (0, 0)))
            u = sum((up[:, k:k + L, :] * conv_w[:, k] for k in range(D_CONV))) + conv_b
            u = jax.nn.silu(u)
            xdbc = u @ x_proj_w.T
            dt = xdbc[..., :DT_RANK]
            Bmat = xdbc[..., DT_RANK:DT_RANK + D_STATE]
            Cmat = xdbc[..., DT_RANK + D_STATE:]
            delta = jax.nn.softplus(dt @ dt_proj_w.T + dt_proj_b)
            A = -jnp.exp(A_log)

            def step(h, ins):
                d_t, B_t, C_t, u_t = ins
                dA = jnp.exp(d_t[:, :, None] * A)
                h = dA * h + (d_t * u_t)[:, :, None] * B_t[:, None, :]
                y = jnp.einsum('bdn,bn->bd', h, C_t)
                return (h, y)
            h0 = jnp.zeros((Bsz, D_INNER, D_STATE), seq.dtype)
            xs = (delta.transpose(1, 0, 2), Bmat.transpose(1, 0, 2), Cmat.transpose(1, 0, 2), u.transpose(1, 0, 2))
            _, ys = jax.lax.scan(step, h0, xs)
            y = ys.transpose(1, 0, 2)
            y = y + u * D
            y = y * jax.nn.silu(z)
            return y
        B, C, H, W = x_feat.shape
        seq = x_feat.reshape(B, C, H * W).transpose(0, 2, 1)
        seq = seq @ to_seq_w.T + to_seq_b
        y = _mamba_forward(seq, in_proj_w, conv_w, conv_b, x_proj_w, dt_proj_w, dt_proj_b, A_log, D)
        seq = y @ out_proj_w.T
        seq = seq @ from_seq_w.T + from_seq_b
        return seq.transpose(0, 2, 1).reshape(B, C, H, W)

    def _gn(v, G=32, eps=1e-5):
        B_, C_, H_, W_ = v.shape
        g = v.reshape(B_, G, C_ // G, H_, W_)
        m = jnp.mean(g, axis=(2, 3, 4), keepdims=True)
        s = jnp.var(g, axis=(2, 3, 4), keepdims=True)
        return ((g - m) / jnp.sqrt(s + eps)).reshape(v.shape)

    def _ln_c(v, eps=1e-6):
        m = jnp.mean(v, axis=1, keepdims=True)
        s = jnp.var(v, axis=1, keepdims=True)
        return (v - m) / jnp.sqrt(s + eps)

    def _ln_t(v, eps=1e-5):
        m = jnp.mean(v, axis=-1, keepdims=True)
        s = jnp.var(v, axis=-1, keepdims=True)
        return (v - m) / jnp.sqrt(s + eps)

    def _to_tokens(v):
        B_, C_, H_, W_ = v.shape
        return v.reshape(B_, C_, H_ * W_).transpose(0, 2, 1)
    def _from_tokens(t, like):
        B_, C_, H_, W_ = like.shape
        return t.transpose(0, 2, 1).reshape(B_, C_, H_, W_)

    x = x + _L0_conv_ref(_gn(x), L0_conv_qkv_w, L0_conv_height_rel, L0_conv_width_rel)
    x = x + _L1_conv_ref(_gn(x), L1_conv_to_seq_w, L1_conv_to_seq_b, L1_conv_in_proj_w, L1_conv_conv_w, L1_conv_conv_b, L1_conv_x_proj_w, L1_conv_dt_proj_w, L1_conv_dt_proj_b, L1_conv_A_log, L1_conv_D, L1_conv_out_proj_w, L1_conv_from_seq_w, L1_conv_from_seq_b)
    return x


_drawn_inputs = setup_inputs


def setup_inputs(seed=0):
    import zlib

    import numpy as np

    out = dict(_drawn_inputs(seed))
    spreads = {'L1_conv_to_seq_b': (0.0, 0.8),
     'L1_conv_conv_b': (0.0, 0.8),
     'L1_conv_D': (1.0, 0.6),
     'L1_conv_from_seq_b': (0.0, 0.1)}
    factors = {'L1_conv_to_seq_w': 8.0,
     'L1_conv_in_proj_w': 8.0,
     'L1_conv_conv_w': 8.0,
     'L1_conv_x_proj_w': 8.0,
     'L1_conv_dt_proj_w': 8.0,
     'L1_conv_dt_proj_b': 8.0,
     'L1_conv_A_log': 8.0,
     'L1_conv_out_proj_w': 8.0,
     'L1_conv_from_seq_w': 8.0}
    for name, (base, spread) in spreads.items():
        noise = np.random.default_rng([zlib.crc32(name.encode()), seed]).standard_normal(out[name].shape)
        drawn = base * np.exp(spread * noise) if base else spread * noise
        out[name] = jnp.asarray(drawn.astype(out[name].dtype))
    for name, factor in factors.items():
        out[name] = (out[name] * factor).astype(out[name].dtype)
    return out
```

```python
from contextlib import ExitStack

import concourse.bass as bass
from concourse import mybir

F32 = mybir.dt.float32
F32R = mybir.dt.float32r
ALU = mybir.AluOpType
ACT = mybir.ActivationFunctionType
AX = mybir.AxisListType

BATCH, C, HH, WW = 2, 256, 64, 64
L = HH * WW
P = 128
KT = C // P
EPS = 1e-5

HEADS, D = 4, 64
SCALE = float(D) ** -0.5
QB = 512
NB = L // QB
QT = QB // P
NKT = L // P
GK = 2
NG = NKT // GK
NCH = L // 512
REL = 2 * WW - 1
YQ = QB // WW
PREP_UNITS = 28
PREP_ACT, PREP_DVE, BLK_POOL = 24, 20, 7

DI, NS, DC, DR = 512, 16, 4, 16
DB = DI // P
T = 512
NC = L // T
GN_DVE = 25


def stand_apart(e, passed):
    e.sem_inc(passed, 1)


def group_norm(nc, role, e, gi, xn, loaded, s, t):
    if role == "vector":
        base = gi * GN_DVE
        e.wait_ge(loaded, 16 * gi + 16)
        for k in range(KT):
            for j in range(L // 512):
                nc.vector.bn_stats(t["st"][:, k, j, :], xn[:, k, j * 512:(j + 1) * 512]).then_inc(s["gn_dve"], 1)
        e.wait_ge(s["gn_dve"], base + 16)
        stand_apart(e, t["passed"])
        for k in range(KT):
            nc.vector.bn_aggr(t["mv"][:, k, :], t["st"][:, k, :, :].rearrange("p a b -> p (a b)")).then_inc(s["gn_dve"], 1)
        e.wait_ge(s["gn_pe"], 2 * gi + 1)
        nc.vector.tensor_copy(t["mg"][:, :, :], t["gps"][:, 0:2 * KT].rearrange("p (k m) -> p k m", k=KT)).then_inc(s["gn_dve"], 1)
        e.wait_ge(s["gn_dve"], base + 19)
        nc.vector.tensor_tensor(t["df"][:, :], t["mv"][:, :, 0], t["mg"][:, :, 0], ALU.subtract).then_inc(s["gn_dve"], 1)
        e.wait_ge(s["gn_dve"], base + 20)
        nc.vector.tensor_tensor(t["sq"][:, :], t["df"][:, :], t["df"][:, :], ALU.mult).then_inc(s["gn_dve"], 1)
        e.wait_ge(s["gn_pe"], 2 * gi + 2)
        nc.vector.scalar_tensor_tensor(out=t["va"][:, :], in0=t["gps"][:, 0:KT], scalar=EPS, in1=t["mg"][:, :, 1],
                                       op0=ALU.add, op1=ALU.add).then_inc(s["gn_dve"], 1)
        e.wait_ge(s["gn_act"], gi + 1)
        nc.vector.reciprocal(t["rs"][:, :], t["sd"][:, :]).then_inc(s["gn_dve"], 1)
        e.wait_ge(s["gn_dve"], base + 23)
        for k in range(KT):
            nc.vector.tensor_scalar(xn[:, k, :], xn[:, k, :], t["mg"][:, k, 0:1], t["rs"][:, k:k + 1],
                                    ALU.subtract, ALU.mult).then_inc(s["gn_dve"], 1)
    elif role == "tensor":
        e.wait_ge(s["gn_dve"], gi * GN_DVE + 18)
        nc.tensor.matmul(t["gps"][:, 0:2 * KT], t["gavg"][:, :], t["mv"][:, :, :].rearrange("p k m -> p (k m)"),
                         start=True, stop=True).then_inc(s["gn_pe"], 1)
        e.wait_ge(s["gn_dve"], gi * GN_DVE + 21)
        nc.tensor.matmul(t["gps"][:, 0:KT], t["gavg"][:, :], t["sq"][:, :], start=True, stop=True).then_inc(s["gn_pe"], 1)
    elif role == "scalar":
        e.wait_ge(s["gn_dve"], gi * GN_DVE + 22)
        nc.scalar.activation(t["sd"][:, :], t["va"][:, :], ACT.Sqrt).then_inc(s["gn_act"], 1)


def gn_tiles(sb, layer):
    return {"st": sb(layer + "_gn_stats", [P, KT, L // 512, 6]), "mv": sb(layer + "_gn_meanvar", [P, KT, 2]),
            "mg": sb(layer + "_gn_group", [P, KT, 2]), "df": sb(layer + "_gn_diff", [P, KT]), "sq": sb(layer + "_gn_square", [P, KT]),
            "va": sb(layer + "_gn_var", [P, KT]), "sd": sb(layer + "_gn_sd", [P, KT]), "rs": sb(layer + "_gn_rstd", [P, KT])}


def attention_layer(nc, x, x1, w_qk, w_v, height_rel, width_rel, key_hot, pos_hot, identity, group_mean):
    with ExitStack() as ctx:
        def sb(name, shape, dt=F32):
            return ctx.enter_context(nc.sbuf_tensor(name, shape, dt))

        def sem(name):
            return ctx.enter_context(nc.semaphore(name))

        xn = sb("a_xn", [P, KT, L])
        k_pos = sb("a_k_pos", [P, L], F32R)
        k_hl = sb("a_k_hl", [P, L], F32R)
        pos = sb("a_pos", [P, L // 2], F32R)
        v_one = sb("a_v_one", [P, NKT, P])
        q_all = sb("a_q", [P, L])
        w_all = sb("a_w", [P, L], F32R)
        m_hi = sb("a_m_hi", [P, 2, QB], F32R)
        m_lo = sb("a_m_lo", [P, 2, QB], F32R)
        m_pos = sb("a_m_pos", [P, 2, 2, QB], F32R)
        q_blk = sb("a_q_blk", [D, 2, QB])
        probs = sb("a_probs", [P, 2, GK, QB])
        w_head = sb("a_w_head", [P, KT, 2, 2, D])
        w_val = sb("a_w_val", [P, KT, C])
        hrel = sb("a_hrel", [D, REL + 1])
        wrel = sb("a_wrel", [D, REL + 1])
        ident = sb("a_ident", [P, P])
        gavg = sb("a_gavg", [P, P])
        col_max = sb("a_col_max", [P, QT, HH])
        row_sum = sb("a_row_sum", [P, QT, HH])
        q_max = sb("a_q_max", [P, QT])
        r_less = sb("a_r_less", [P, QT, 3 * D])
        rec = sb("a_rec", [D, QB])
        out_n = sb("a_out_n", [D, QB])
        x_res = sb("a_x_res", [D, 2, QB])
        t = gn_tiles(sb, "a")
        t["gavg"] = gavg

        sc = ctx.enter_context(nc.psum_tensor("a_scores", [P, 2, GK, QB], F32))
        mx = ctx.enter_context(nc.psum_tensor("a_mx", [P, 2, 512], F32))
        oa = ctx.enter_context(nc.psum_tensor("a_oa", [P, QB], F32))
        mi = ctx.enter_context(nc.psum_tensor("a_mi", [P, 512], F32))
        t["gps"] = mi
        rh = mi[:, 0:QT * 66].rearrange("p (t r) -> p t r", t=QT)

        s = {n: sem("a_" + n) for n in ("gn_dve", "gn_pe", "gn_act")}
        const_in, x_in, wh_in = (sem("a_" + n) for n in ("const_in", "x_in", "wh_in"))
        res_in, x1_out = ([sem(f"a_{n}{k}") for k in range(2)] for n in ("res_in", "x1_out"))
        ones_set, hot_in = sem("a_ones_set"), sem("a_hot_in")
        passed = t["passed"] = sem("a_passed")
        proj_mm, prep_act, prep_dve, prep_pool = (sem("a_" + n) for n in ("proj_mm", "prep_act", "prep_dve", "prep_pool"))
        blk_pool, mx_mm, mx_red, rh_mm, sum_dve, max_dve, rp_dve, tr_mm, hi_act, lo_dve = (
            sem("a_" + n) for n in ("blk_pool", "mx_mm", "mx_red", "rh_mm", "sum_dve", "max_dve", "rp_dve", "tr_mm",
                                    "hi_act", "lo_dve"))
        score_mm, exp_act, pv_mm, rec_dve, oa_read, out_dve = (
            sem("a_" + n) for n in ("score_mm", "exp_act", "pv_mm", "rec_dve", "oa_read", "out_dve"))
        N_CONST = 5

        def unit_bank(u):
            return sc[:, (u % 4) // 2, u % 2, :]

        def main_blocks(e, body):
            with e.Fori(0, NB // 2 - 1) as ii:
                body(ii, 0, True)
                body(ii, 1, True)
            body(NB // 2 - 1, 0, True)
            body(NB // 2 - 1, 1, False)

        block = ctx.enter_context(nc.Block())

        @block.sync
        def _(sp):
            for dst, src in ((w_val[:, :, :], w_v), (hrel[:, 0:REL], height_rel), (wrel[:, 0:REL], width_rel),
                             (ident[:, :], identity), (gavg[:, :], group_mean)):
                sp.dma_start(dst, src).then_inc(const_in, 16)
            with sp.Fori(0, BATCH) as b:
                sp.wait_ge(proj_mm, b * (HEADS * PREP_UNITS))
                sp.dma_start(xn[:, :, :], x[bass.ds(b, 1), :, :].rearrange("o (k p) l -> (o p) k l", p=P)).then_inc(x_in, 16)
                with sp.Fori(0, HEADS) as h:
                    H = b * HEADS + h
                    sp.wait_ge(proj_mm, H * PREP_UNITS)
                    for k in range(KT):
                        for dup in range(2):
                            sp.dma_start(w_head[:, k, :, dup, :], w_qk[k * P:(k + 1) * P, bass.ds(h, 1), :, :]
                                         .rearrange("p o r d -> p (o r) d")).then_inc(wh_in, 16)
                    for i in range(NB):
                        sp.wait_ge(x1_out[i % 2], H * (8 * NB) + 16 * (i // 2))
                        sp.dma_start(x_res[:, i % 2, :], x[bass.ds(b, 1), bass.ds(h * D, D), i * QB:(i + 1) * QB]
                                     .rearrange("o c l -> (o c) l")).then_inc(res_in[i % 2], 16)
            for k in range(2):
                sp.wait_ge(x1_out[k], 8 * BATCH * HEADS * NB)

        @block.gpsimd
        def _(pool):
            pool.dma_start(pos[:, :], pos_hot).then_inc(hot_in, 16)
            pool.dma_start(k_pos[D:P, :], key_hot).then_inc(hot_in, 16)
            nc.gpsimd.memset(v_one[:, :, D:P], 1.0).then_inc(ones_set, 1)
            nc.gpsimd.memset(r_less[:, :, 0:D], 0.0).then_inc(ones_set, 1)

            def block_operands(H, i, sl):
                blk = bass.ds(i * QB, QB)
                B = H * NB + i
                cp = nc.gpsimd.tensor_copy
                stand_apart(pool, passed)
                cp(q_blk[:, sl, :], q_all[0:D, blk]).then_inc(blk_pool, 1)
                cp(m_hi[0:D, sl, :], q_all[0:D, blk]).then_inc(blk_pool, 1)
                cp(m_lo[D:P, sl, :], q_all[D:P, blk]).then_inc(blk_pool, 1)
                cp(m_hi[D:P, sl, :], w_all[D:P, blk]).then_inc(blk_pool, 1)
                for half in range(2):
                    cp(m_pos[0:D, sl, half, :], w_all[0:D, blk]).then_inc(blk_pool, 1)
                pool.wait_ge(blk_pool, B * BLK_POOL + 2)
                stand_apart(pool, passed)
                nc.gpsimd.tensor_tensor(m_lo[0:D, sl, :], q_all[0:D, blk], m_hi[0:D, sl, :], ALU.subtract).then_inc(blk_pool, 1)

            with pool.Fori(0, BATCH) as b:
                with pool.Fori(0, HEADS) as h:
                    H = b * HEADS + h
                    for c in range(NCH):
                        pool.wait_ge(prep_act, H * PREP_ACT + c + 1)
                        stand_apart(pool, passed)
                        nc.gpsimd.tensor_copy(k_pos[0:D, c * 512:(c + 1) * 512], k_hl[0:D, c * 512:(c + 1) * 512]).then_inc(prep_pool, 1)
                    pool.wait_ge(prep_act, H * PREP_ACT + PREP_ACT)
                    pool.wait_ge(prep_dve, H * PREP_DVE + PREP_DVE)
                    block_operands(H, 0, 0)

                    def body(ii, sl, nxt):
                        i = 2 * ii + sl
                        B = H * NB + i
                        if nxt:
                            pool.wait_ge(pv_mm, B * NG)
                            block_operands(H, i + 1, 1 - sl)
                        pool.wait_ge(out_dve, B + 1)
                        blk = bass.ds(i * QB, QB)
                        pool.dma_start(x1[bass.ds(b, 1), bass.ds(h * D, D), blk].rearrange("o c l -> (o c) l"),
                                       x_res[:, sl, :]).then_inc(x1_out[sl], 16)

                    main_blocks(pool, body)

        @block.scalar
        def _(act):
            with act.Fori(0, BATCH) as b:
                group_norm(nc, "scalar", act, b, xn, x_in, s, t)
                with act.Fori(0, HEADS) as h:
                    H = b * HEADS + h
                    for u in range(8):
                        act.wait_ge(proj_mm, H * PREP_UNITS + u + 1)
                        nc.scalar.activation(k_hl[:, u * 512:(u + 1) * 512], unit_bank(u), ACT.Copy, scale=SCALE).then_inc(prep_act, 1)
                    for u in range(8, 16):
                        act.wait_ge(proj_mm, H * PREP_UNITS + u + 1)
                        nc.scalar.activation(q_all[:, (u - 8) * 512:(u - 7) * 512], unit_bank(u), ACT.Copy).then_inc(prep_act, 1)
                    for u in range(20, 28):
                        act.wait_ge(proj_mm, H * PREP_UNITS + u + 1)
                        nc.scalar.activation(w_all[:, :].rearrange("p (y x) -> p x y", x=WW)[:, 8 * (u - 20):8 * (u - 19), :],
                                             unit_bank(u).rearrange("p (x y) -> p x y", x=8), ACT.Copy).then_inc(prep_act, 1)

                    def r_hi(B, sl):
                        act.wait_ge(tr_mm, B + 1)
                        nc.scalar.activation(m_pos[D:P, sl, :, :], mx[D:P, :, :], ACT.Copy).then_inc(hi_act, 1)

                    r_hi(H * NB, 0)

                    def body(ii, sl, nxt):
                        i = 2 * ii + sl
                        B = H * NB + i
                        for g in range(NG):
                            act.wait_ge(score_mm, B * NG + g + 1)
                            nc.scalar.activation(probs[:, g % 2, :, :], sc[:, g % 2, :, :], ACT.Exp).then_inc(exp_act, 1)
                            if g == 13 and nxt:
                                r_hi(B + 1, 1 - sl)

                    main_blocks(act, body)

        @block.vector
        def _(dve):
            with dve.Fori(0, BATCH) as b:
                group_norm(nc, "vector", dve, b, xn, x_in, s, t)
                with dve.Fori(0, HEADS) as h:
                    H = b * HEADS + h
                    for u in range(8):
                        dve.wait_ge(prep_act, H * PREP_ACT + u + 1)
                        sl_ = slice(u * 512, (u + 1) * 512)
                        nc.vector.scalar_tensor_tensor(out=k_hl[D:P, sl_], in0=unit_bank(u)[D:P, :], scalar=SCALE,
                                                       in1=k_hl[D:P, sl_], op0=ALU.mult, op1=ALU.subtract).then_inc(prep_dve, 1)
                    for u in range(16, 20):
                        dve.wait_ge(proj_mm, H * PREP_UNITS + u + 1)
                        if u == 16:
                            dve.wait_ge(ones_set, 1)
                        nc.vector.tensor_copy(v_one[:, 8 * (u - 16):8 * (u - 15), 0:D],
                                              unit_bank(u).rearrange("p (t d) -> p t d", t=8)).then_inc(prep_dve, 1)
                    for u in range(20, 28):
                        dve.wait_ge(prep_act, H * PREP_ACT + u - 4 + 1)
                        w_ap = w_all[0:D, :].rearrange("p (y x) -> p x y", x=WW)[:, 8 * (u - 20):8 * (u - 19), :]
                        nc.vector.tensor_tensor(w_ap, unit_bank(u)[0:D, :].rearrange("p (x y) -> p x y", x=8), w_ap,
                                                ALU.subtract).then_inc(prep_dve, 1)

                    def block_max(B, sl):
                        for k in range(QT * NCH):
                            qt, c = divmod(k, NCH)
                            dve.wait_ge(mx_mm, B * (QT * NCH) + k + 1)
                            nc.vector.tensor_reduce(col_max[:, qt, c * 8:(c + 1) * 8],
                                                    mx[:, k % 2, :].rearrange("p (y x) -> p y x", x=WW), AX.X, ALU.max).then_inc(mx_red, 1)
                        dve.wait_ge(rh_mm, B + 1)
                        dve.wait_ge(mx_red, B * (QT * NCH) + QT * NCH)
                        for half in range(2):
                            r = slice(half * D, half * D + D)
                            nc.vector.tensor_tensor(row_sum[r, :, :], rh[r, :, 1 - half:1 - half + HH], col_max[r, :, :], ALU.add).then_inc(sum_dve, 1)
                        dve.wait_ge(sum_dve, 2 * B + 2)
                        nc.vector.tensor_reduce(q_max[:, :], row_sum[:, :, :], AX.X, ALU.max).then_inc(max_dve, 1)
                        dve.wait_ge(max_dve, B + 1)
                        for half in range(2):
                            r = slice(half * D, half * D + D)
                            for kh in range(2):
                                c0 = 1 - half + kh * 32
                                nc.vector.tensor_tensor(r_less[r, :, D + kh * D:2 * D + kh * D].rearrange("p t (a y) -> p t a y", a=2),
                                                        rh[r, :, c0:c0 + 32].unsqueeze(2).to_broadcast([D, QT, 2, 32]),
                                                        q_max[r, :].unsqueeze(2).unsqueeze(3).to_broadcast([D, QT, 2, 32]),
                                                        ALU.subtract).then_inc(rp_dve, 1)
                        dve.wait_ge(hi_act, B + 1)
                        nc.vector.tensor_tensor(m_pos[96:P, sl, :, :], mx[96:P, :, :], m_pos[96:P, sl, :, :], ALU.subtract).then_inc(lo_dve, 1)

                    block_max(H * NB, 0)

                    def body(ii, sl, nxt):
                        i = 2 * ii + sl
                        B = H * NB + i
                        if nxt:
                            block_max(B + 1, 1 - sl)
                        dve.wait_ge(pv_mm, B * NG + NG)
                        nc.vector.reciprocal(rec[:, :], oa[D:P, :]).then_inc(rec_dve, 1)
                        dve.wait_ge(rec_dve, B + 1)
                        nc.vector.tensor_tensor(out_n[:, :], oa[0:D, :], rec[:, :], ALU.mult).then_inc(oa_read, 1)
                        dve.wait_ge(oa_read, B + 1)
                        dve.wait_ge(res_in[sl], H * (8 * NB) + 16 * ii + 16)
                        nc.vector.tensor_tensor(x_res[:, sl, :], out_n[:, :], x_res[:, sl, :], ALU.add).then_inc(out_dve, 1)

                    main_blocks(dve, body)

        @block.tensor
        def _(pe):
            pe.wait_ge(const_in, 16 * N_CONST)
            pe.wait_ge(hot_in, 32)
            pe.wait_ge(ones_set, 2)
            with pe.Fori(0, BATCH) as b:
                group_norm(nc, "tensor", pe, b, xn, x_in, s, t)
                pe.wait_ge(s["gn_dve"], b * GN_DVE + GN_DVE)
                stand_apart(pe, passed)
                with pe.Fori(0, HEADS) as h:
                    H = b * HEADS + h
                    pe.wait_ge(wh_in, H * 64 + 64)
                    pe.wait_ge(exp_act, H * (NB * NG))

                    def bank_free(u):
                        v = u - 4
                        if v < 0:
                            return
                        if v < 8:
                            pe.wait_ge(prep_dve, H * PREP_DVE + v + 1)
                        elif v < 16:
                            pe.wait_ge(prep_act, H * PREP_ACT + v + 1)
                        else:
                            pe.wait_ge(prep_dve, H * PREP_DVE + v - 8 + 1)

                    for u in range(16):
                        bank_free(u)
                        role, c = (1, u) if u < 8 else (0, u - 8)
                        for k in range(KT):
                            mm = nc.tensor.matmul(unit_bank(u), w_head[:, k, role, :, :].rearrange("p a d -> p (a d)"),
                                                  xn[:, k, c * 512:(c + 1) * 512], start=(k == 0), stop=(k == KT - 1))
                        mm.then_inc(proj_mm, 1)
                    for u in range(16, 20):
                        bank_free(u)
                        for j in range(8):
                            tok = slice(((u - 16) * 8 + j) * P, ((u - 16) * 8 + j + 1) * P)
                            for k in range(KT):
                                mm = nc.tensor.matmul(unit_bank(u)[:, j * D:(j + 1) * D], xn[:, k, tok],
                                                      w_val[:, k, bass.ds(h * D, D)], start=(k == 0), stop=(k == KT - 1))
                        mm.then_inc(proj_mm, 1)
                    pe.wait_ge(prep_act, H * PREP_ACT + 16)
                    for u in range(20, 28):
                        bank_free(u)
                        stand_apart(pe, passed)
                        for j in range(8):
                            xq = (u - 20) * 8 + j
                            for half in range(2):
                                mm = nc.tensor.matmul(unit_bank(u)[half * D:half * D + D, j * HH:(j + 1) * HH],
                                                      wrel[:, WW - 1 - xq:2 * WW - 1 - xq],
                                                      q_all[0:D, :].rearrange("p (y x) -> p x y", x=WW)[:, xq, :],
                                                      start=True, stop=True)
                        mm.then_inc(proj_mm, 1)

                    def height_logits(B, i, sl):
                        pe.wait_ge(blk_pool, B * BLK_POOL + BLK_POOL)
                        pe.wait_ge(rp_dve, 4 * B)
                        for qt in range(QT):
                            r0 = WW - 2 - 2 * qt - i * YQ
                            win = hrel[:, bass.ds(r0, HH + 1)]
                            mm = nc.tensor.matmul(rh[:, qt, 0:HH + 1], q_blk[:, sl, qt * P:(qt + 1) * P], win, start=True, stop=True)
                        mm.then_inc(rh_mm, 1)

                    def max_scores(B, sl, ks):
                        for k in ks:
                            qt, c = divmod(k, NCH)
                            if k < 2:
                                pe.wait_ge(lo_dve, B)
                            else:
                                pe.wait_ge(mx_red, B * (QT * NCH) + k - 1)
                            nc.tensor.matmul(mx[:, k % 2, :], m_hi[:, sl, qt * P:(qt + 1) * P], k_pos[:, c * 512:(c + 1) * 512],
                                             start=True, stop=True).then_inc(mx_mm, 1)

                    def turn(B):
                        pe.wait_ge(rp_dve, 4 * B + 4)
                        for half in range(2):
                            for qt in range(QT):
                                mm = nc.tensor.transpose(mx[:, half, qt * P:(qt + 1) * P],
                                                         r_less[:, qt, half * D:half * D + P],
                                                         ident[:, :])
                        mm.then_inc(tr_mm, 1)

                    pe.wait_ge(prep_pool, H * NCH + NCH)
                    height_logits(H * NB, 0, 0)
                    max_scores(H * NB, 0, range(QT * NCH))
                    turn(H * NB)
                    pe.wait_ge(prep_dve, H * PREP_DVE + PREP_DVE)
                    stand_apart(pe, passed)

                    def body(ii, sl, nxt):
                        i = 2 * ii + sl
                        B = H * NB + i

                        def weigh(g):
                            pe.wait_ge(exp_act, B * NG + g + 1)
                            if g == 0:
                                pe.wait_ge(oa_read, B)
                            for j in range(GK):
                                kt = g * GK + j
                                mm = nc.tensor.matmul(oa[:, :], v_one[:, kt, :], probs[:, g % 2, j, :],
                                                      start=(kt == 0), stop=(kt == NKT - 1))
                            mm.then_inc(pv_mm, 1)

                        pe.wait_ge(lo_dve, B + 1)
                        for g in range(NG):
                            for j in range(GK):
                                kt = g * GK + j
                                keys = slice(kt * P, (kt + 1) * P)
                                half, kp = divmod(kt, NKT // 2)
                                nc.tensor.matmul(sc[:, g % 2, j, :], k_pos[:, keys], m_hi[:, sl, :], start=True, stop=False)
                                nc.tensor.matmul(sc[:, g % 2, j, :], k_hl[:, keys], m_lo[:, sl, :], start=False, stop=False)
                                mm = nc.tensor.matmul(sc[:, g % 2, j, :], pos[:, kp * P:(kp + 1) * P], m_pos[:, sl, half, :],
                                                      start=False, stop=True)
                            mm.then_inc(score_mm, 1)
                            if nxt:
                                if g == 0:
                                    height_logits(B + 1, i + 1, 1 - sl)
                                max_scores(B + 1, 1 - sl, range(3 * g, min(3 * g + 3, QT * NCH)))
                                if g == 13:
                                    turn(B + 1)
                            if g >= 1:
                                weigh(g - 1)
                        weigh(NG - 1)

                    main_blocks(pe, body)


def mamba_layer(nc, x1, out, w_to, b_to, w_in, conv_w, conv_b, w_x, w_dt, b_dt, a_log, d_skip, w_out, w_from, b_from,
                identity, group_mean, pick):
    with ExitStack() as ctx:
        def sb(name, shape, dt=F32):
            return ctx.enter_context(nc.sbuf_tensor(name, shape, dt))

        def sem(name):
            return ctx.enter_context(nc.semaphore(name))

        xn = sb("m_xn", [P, KT, L])
        seq = sb("m_seq", [P, KT, T])
        u_raw = sb("m_u_raw", [P, DB, DC - 1 + T])
        u_conv = sb("m_u_conv", [P, DB, T])
        u_act = sb("m_u_act", [P, DB, T])
        z_act = sb("m_z_act", [P, DB, T])
        delta = sb("m_delta", [P, DB, T])
        du = sb("m_du", [P, DB, T])
        bc = sb("m_bc", [2 * 2 * NS, T], F32R)
        dt_low = sb("m_dt_low", [5 * NS, T])
        bc_all = sb("m_bc_all", [P, 2, 2, T])
        d_a = sb("m_d_a", [P, 2, DB, T])
        d_bu = sb("m_d_bu", [P, 2, DB, T])
        h = sb("m_h", [P, 2, DB, T])
        hc = sb("m_hc", [P, 2, DB, T])
        state = sb("m_state", [P, DB, NS])
        o_in = sb("m_o_in", [P, KT, T])
        x_res = sb("m_x_res", [P, KT, T])
        s_to, s_in = sb("m_w_to", [P, KT, C]), sb("m_w_in", [P, KT, 2 * DI])
        s_x, s_dt = sb("m_w_x", [P, DB, 5 * NS]), sb("m_w_dt", [5 * NS, DI])
        s_out, s_from = sb("m_w_out", [P, DB, C]), sb("m_w_from", [P, KT, C])
        s_bto, s_bfrom = sb("m_b_to", [P, KT]), sb("m_b_from", [P, KT])
        s_cw, s_cb, s_bdt, s_d = sb("m_conv_w", [P, DB, DC]), sb("m_conv_b", [P, DB]), sb("m_b_dt", [P, DB]), sb("m_d", [P, DB])
        a_exp, a_neg = sb("m_a_exp", [P, DB, NS]), sb("m_a_neg", [P, DB, NS])
        ident, gavg = sb("m_ident", [P, P]), sb("m_gavg", [P, P])
        s_pick = sb("m_pick", [2 * 2 * NS, 2 * NS, P], F32R)
        t = gn_tiles(sb, "m")
        t["gavg"] = gavg
        v_dt, v_abs, e_abs, one_e, log_e, low_e = hc[:, 0], hc[:, 1], d_a[:, 0], d_a[:, 1], d_bu[:, 0], d_bu[:, 1]

        yp = ctx.enter_context(nc.psum_tensor("m_yp", [P, DB, T], F32))
        wk = ctx.enter_context(nc.psum_tensor("m_wk", [P, 4, T], F32))
        t["gps"] = wk[:, 3, :]

        s = {n: sem("m_" + n) for n in ("gn_dve", "gn_pe", "gn_act")}
        const_in, hot_in, x_in, res_in, out_out = (sem("m_" + n) for n in ("const_in", "hot_in", "x_in", "res_in", "out_out"))
        wk_mm, wk_act, wk_dve = sem("m_wk_mm"), sem("m_wk_act"), sem("m_wk_dve")
        halo, conv, act_u, sp_act, sp_dve, du_dve = (sem("m_" + n) for n in ("halo", "conv", "act_u", "sp_act", "sp_dve", "du_dve"))
        a_act, a_dve, state0 = sem("m_a_act"), sem("m_a_dve"), sem("m_state0")
        passed = t["passed"] = sem("m_passed")
        da_act, dbu, scan, st_dve, hc_done, y_mm, y_dve = (
            sem("m_" + n) for n in ("da_act", "dbu", "scan", "st_dve", "hc_done", "y_mm", "y_dve"))

        SEQ, U, Z, XD, DT, BC, OUT, FROM = 0, 2, 6, 10, 11, 15, 47, 49
        UNITS = 51
        reader = ["dve"] * 2 + ["act"] * 8 + ["dve"] * 5 + ["act"] * 34 + ["dve"] * 2
        READS = {"act": UNITS - 9 + 1, "dve": 9}

        def reads(who, u):
            return sum(reader[v] == who or (who == "act" and v == XD) for v in range(u + 1))

        def bank(u):
            return wk[:, u % 4, :]

        def bank_free(pe, CH, u):
            if u >= 4:
                w = reader[u - 4]
                pe.wait_ge(wk_act if w == "act" else wk_dve, CH * READS[w] + reads(w, u - 4))
            elif u == 0:
                pe.wait_ge(wk_dve, CH * READS["dve"])
                pe.wait_ge(wk_act, CH * READS["act"])

        block = ctx.enter_context(nc.Block())

        consts = [(s_to, w_to), (s_in, w_in), (s_x, w_x), (s_out, w_out), (s_from, w_from), (s_bto, b_to), (s_bfrom, b_from),
                  (s_cw, conv_w), (s_cb, conv_b), (s_bdt, b_dt), (s_d, d_skip), (a_exp, a_log), (ident, identity), (gavg, group_mean)]

        def all_of(tile):
            return tile[tuple(slice(None) for _ in tile.shape)]

        @block.sync
        def _(sp):
            for dst, src in consts:
                sp.dma_start(all_of(dst), src).then_inc(const_in, 16)
            sp.dma_start(s_dt[4 * NS:5 * NS, :], w_dt).then_inc(const_in, 16)
            with sp.Fori(0, BATCH) as b:
                sp.wait_ge(wk_mm, b * (NC * UNITS))
                sp.dma_start(xn[:, :, :], x1[bass.ds(b, 1), :, :].rearrange("o (k p) l -> (o p) k l", p=P)).then_inc(x_in, 16)
                with sp.Fori(0, NC) as c:
                    CH = b * NC + c
                    sp.wait_ge(out_out, CH * 16)
                    sp.dma_start(x_res[:, :, :], x1[bass.ds(b, 1), :, bass.ds(c * T, T)].rearrange("o (k p) l -> (o p) k l", p=P)).then_inc(res_in, 16)
                    sp.wait_ge(wk_dve, CH * READS["dve"] + READS["dve"])
                    sp.dma_start(out[bass.ds(b, 1), :, bass.ds(c * T, T)].rearrange("o (k p) l -> (o p) k l", p=P), x_res[:, :, :]).then_inc(out_out, 16)
            sp.wait_ge(out_out, 16 * BATCH * NC)

        @block.gpsimd
        def _(pool):
            pool.dma_start(s_pick[:, :, :], pick).then_inc(hot_in, 16)
            with pool.Fori(0, BATCH) as b:
                with pool.Fori(0, NC) as c:
                    CH = b * NC + c
                    pool.wait_ge(du_dve, CH + 1)
                    for n in range(NS):
                        pool.wait_ge(wk_act, CH * READS["act"] + reads("act", BC + 2 * n))
                        if n >= 2:
                            pool.wait_ge(scan, CH * (NS * DB) + (n - 1) * DB)
                        nc.gpsimd.tensor_tensor(d_bu[:, n % 2, :, :], du[:, :, :],
                                                bc_all[:, n % 2, 0:1, :].to_broadcast([P, DB, T]), ALU.mult).then_inc(dbu, 1)

        @block.scalar
        def _(act):
            act.wait_ge(const_in, 16 * (len(consts) + 1))
            nc.scalar.activation(a_exp[:, :, :], a_exp[:, :, :], ACT.Exp).then_inc(a_act, 1)
            with act.Fori(0, BATCH) as b:
                group_norm(nc, "scalar", act, b, xn, x_in, s, t)
                with act.Fori(0, NC) as c:
                    CH = b * NC + c
                    act.wait_ge(halo, CH + b + 1)
                    for k in range(DB):
                        act.wait_ge(wk_mm, CH * UNITS + U + k + 1)
                        nc.scalar.activation(u_raw[:, k, DC - 1:], bank(U + k), ACT.Copy).then_inc(wk_act, 1)
                    for k in range(DB):
                        act.wait_ge(wk_mm, CH * UNITS + Z + k + 1)
                        nc.scalar.activation(z_act[:, k, :], bank(Z + k), ACT.Silu).then_inc(wk_act, 1)
                    act.wait_ge(conv, (CH + 1) * (DB * DC))
                    nc.scalar.activation(u_act[:, :, :], u_conv[:, :, :], ACT.Silu).then_inc(act_u, 1)
                    act.wait_ge(wk_mm, CH * UNITS + XD + 1)
                    nc.scalar.activation(dt_low[4 * NS:5 * NS, :], bank(XD)[4 * NS:5 * NS, :], ACT.Copy).then_inc(act_u, 1)
                    nc.scalar.activation(bc[:, :], bank(XD)[0:4 * NS, :], ACT.Copy).then_inc(wk_act, 1)
                    act.wait_ge(wk_dve, CH * READS["dve"] + reads("dve", DT + DB - 1))
                    nc.scalar.activation(v_abs, v_dt, ACT.Abs).then_inc(sp_act, 1)
                    act.wait_ge(sp_act, 3 * CH + 1)
                    nc.scalar.activation(e_abs, v_abs, ACT.Exp, scale=-1.0).then_inc(sp_act, 1)
                    act.wait_ge(sp_dve, 4 * CH + 1)
                    nc.scalar.activation(log_e, one_e, ACT.Ln).then_inc(sp_act, 1)
                    act.wait_ge(sp_dve, 4 * CH + 4)
                    act.wait_ge(a_dve, 1)
                    act.wait_ge(du_dve, CH + 1)
                    for n in range(NS):
                        for k in range(2):
                            act.wait_ge(wk_mm, CH * UNITS + BC + 2 * n + k + 1)
                            if n >= 2:
                                if k == 0:
                                    act.wait_ge(dbu, CH * NS + n - 1)
                                else:
                                    act.wait_ge(hc_done, CH * NS + n - 1)
                            nc.scalar.activation(bc_all[:, n % 2, k, :], bank(BC + 2 * n + k), ACT.Copy).then_inc(wk_act, 1)
                        if n >= 2:
                            act.wait_ge(scan, CH * (NS * DB) + (n - 1) * DB)
                        for k in range(DB):
                            nc.scalar.activation(d_a[:, n % 2, k, :], delta[:, k, :], ACT.Exp, scale=a_neg[:, k, n:n + 1]).then_inc(da_act, 1)
                    for k in range(KT):
                        act.wait_ge(wk_mm, CH * UNITS + OUT + k + 1)
                        nc.scalar.activation(o_in[:, k, :], bank(OUT + k), ACT.Copy).then_inc(wk_act, 1)

        @block.vector
        def _(dve):
            dve.wait_ge(a_act, 1)
            nc.vector.tensor_scalar(a_neg[:, :, :], a_exp[:, :, :], -1.0, None, ALU.mult).then_inc(a_dve, 1)
            with dve.Fori(0, BATCH) as b:
                group_norm(nc, "vector", dve, b, xn, x_in, s, t)
                nc.vector.memset(state[:, :, :], 0.0).then_inc(state0, 1)
                nc.vector.memset(u_raw[:, :, 0:DC - 1], 0.0).then_inc(halo, 1)
                with dve.Fori(0, NC) as c:
                    CH = b * NC + c
                    for k in range(KT):
                        dve.wait_ge(wk_mm, CH * UNITS + SEQ + k + 1)
                        nc.vector.tensor_scalar(seq[:, k, :], bank(SEQ + k), s_bto[:, k:k + 1], None, ALU.add).then_inc(wk_dve, 1)
                    dve.wait_ge(wk_act, CH * READS["act"] + reads("act", U + DB - 1))
                    for tap in range(DC):
                        for k in range(DB):
                            src = u_raw[:, k, tap:tap + T]
                            if tap == 0:
                                nc.vector.tensor_scalar(u_conv[:, k, :], src, s_cw[:, k, 0:1], s_cb[:, k:k + 1],
                                                        ALU.mult, ALU.add).then_inc(conv, 1)
                            else:
                                dve.wait_ge(conv, CH * (DB * DC) + (tap - 1) * DB + k + 1)
                                nc.vector.scalar_tensor_tensor(out=u_conv[:, k, :], in0=src, scalar=s_cw[:, k, tap:tap + 1],
                                                               in1=u_conv[:, k, :], op0=ALU.mult, op1=ALU.add).then_inc(conv, 1)
                    nc.vector.tensor_copy(u_raw[:, :, 0:DC - 1], u_raw[:, :, T:T + DC - 1]).then_inc(halo, 1)
                    dve.wait_ge(wk_act, CH * READS["act"] + reads("act", XD))
                    nc.vector.tensor_tensor(bc[2 * NS:4 * NS, :], bank(XD)[2 * NS:4 * NS, :], bc[2 * NS:4 * NS, :],
                                            ALU.subtract).then_inc(wk_dve, 1)
                    for k in range(DB):
                        dve.wait_ge(wk_mm, CH * UNITS + DT + k + 1)
                        nc.vector.tensor_scalar(v_dt[:, k, :], bank(DT + k), s_bdt[:, k:k + 1], None, ALU.add).then_inc(wk_dve, 1)
                    dve.wait_ge(sp_act, 3 * CH + 2)
                    nc.vector.tensor_scalar(one_e, e_abs, 1.0, None, ALU.add).then_inc(sp_dve, 1)
                    dve.wait_ge(sp_dve, 4 * CH + 1)
                    nc.vector.scalar_tensor_tensor(out=low_e, in0=one_e, scalar=1.0, in1=e_abs, op0=ALU.subtract,
                                                   op1=ALU.subtract).then_inc(sp_dve, 1)
                    dve.wait_ge(sp_act, 3 * CH + 3)
                    dve.wait_ge(sp_dve, 4 * CH + 2)
                    nc.vector.tensor_tensor(log_e, log_e, low_e, ALU.subtract).then_inc(sp_dve, 1)
                    dve.wait_ge(sp_dve, 4 * CH + 3)
                    nc.vector.scalar_tensor_tensor(out=delta[:, :, :], in0=v_dt, scalar=0.0, in1=log_e, op0=ALU.max,
                                                   op1=ALU.add).then_inc(sp_dve, 1)
                    dve.wait_ge(sp_dve, 4 * CH + 4)
                    nc.vector.tensor_tensor(du[:, :, :], delta[:, :, :], u_act[:, :, :], ALU.mult).then_inc(du_dve, 1)
                    for n in range(NS):
                        dve.wait_ge(dbu, CH * NS + n + 1)
                        if n == 0:
                            dve.wait_ge(st_dve, CH * NS)
                            dve.wait_ge(state0, b + 1)
                        for k in range(DB):
                            dve.wait_ge(da_act, CH * (NS * DB) + n * DB + k + 1)
                            nc.vector.tensor_tensor_scan(h[:, n % 2, k, :], d_a[:, n % 2, k, :], d_bu[:, n % 2, k, :],
                                                         state[:, k, n:n + 1], ALU.mult, ALU.add).then_inc(scan, 1)
                        if n >= 2:
                            dve.wait_ge(y_mm, CH * NS + n - 1)
                        dve.wait_ge(scan, CH * (NS * DB) + (n + 1) * DB)
                        dve.wait_ge(wk_act, CH * READS["act"] + reads("act", BC + 2 * n + 1))
                        nc.vector.tensor_tensor(hc[:, n % 2, :, :], h[:, n % 2, :, :],
                                                bc_all[:, n % 2, 1:2, :].to_broadcast([P, DB, T]), ALU.mult).then_inc(hc_done, 1)
                        nc.vector.tensor_copy(state[:, :, n], h[:, n % 2, :, T - 1]).then_inc(st_dve, 1)
                    dve.wait_ge(y_mm, CH * NS + NS)
                    for k in range(DB):
                        nc.vector.scalar_tensor_tensor(out=u_conv[:, k, :], in0=u_act[:, k, :], scalar=s_d[:, k:k + 1],
                                                       in1=yp[:, k, :], op0=ALU.mult, op1=ALU.add).then_inc(y_dve, 1)
                    dve.wait_ge(y_dve, CH * (DB + 1) + DB)
                    nc.vector.tensor_tensor(u_conv[:, :, :], u_conv[:, :, :], z_act[:, :, :], ALU.mult).then_inc(y_dve, 1)
                    dve.wait_ge(res_in, 16 * CH + 16)
                    for k in range(KT):
                        dve.wait_ge(wk_mm, CH * UNITS + FROM + k + 1)
                        nc.vector.scalar_tensor_tensor(out=x_res[:, k, :], in0=bank(FROM + k), scalar=s_bfrom[:, k:k + 1],
                                                       in1=x_res[:, k, :], op0=ALU.add, op1=ALU.add).then_inc(wk_dve, 1)

        @block.tensor
        def _(pe):
            pe.wait_ge(const_in, 16 * (len(consts) + 1))
            pe.wait_ge(hot_in, 16)
            with pe.Fori(0, BATCH) as b:
                group_norm(nc, "tensor", pe, b, xn, x_in, s, t)
                pe.wait_ge(s["gn_dve"], b * GN_DVE + GN_DVE)
                stand_apart(pe, passed)
                with pe.Fori(0, NC) as c:
                    CH = b * NC + c

                    def project(first, w, src, m_tiles, k_tiles):
                        for m in range(m_tiles):
                            bank_free(pe, CH, first + m)
                            for k in range(k_tiles):
                                mm = nc.tensor.matmul(bank(first + m), w[:, k, m * P:(m + 1) * P], src(k),
                                                      start=(k == 0), stop=(k == k_tiles - 1))
                            mm.then_inc(wk_mm, 1)

                    project(SEQ, s_to, lambda k: xn[:, k, bass.ds(c * T, T)], KT, KT)
                    pe.wait_ge(wk_dve, CH * READS["dve"] + reads("dve", SEQ + 1))
                    project(U, s_in, lambda k: seq[:, k, :], 2 * DB, KT)
                    pe.wait_ge(act_u, 2 * CH + 1)
                    bank_free(pe, CH, XD)
                    for k in range(DB):
                        mm = nc.tensor.matmul(bank(XD)[0:5 * NS, :], s_x[:, k, :], u_act[:, k, :], start=(k == 0), stop=(k == DB - 1))
                    mm.then_inc(wk_mm, 1)
                    pe.wait_ge(act_u, 2 * CH + 2)
                    for m in range(DB):
                        bank_free(pe, CH, DT + m)
                        nc.tensor.matmul(bank(DT + m), s_dt[4 * NS:5 * NS, m * P:(m + 1) * P], dt_low[4 * NS:5 * NS, :],
                                         start=True, stop=True).then_inc(wk_mm, 1)
                    pe.wait_ge(wk_dve, CH * READS["dve"] + reads("dve", XD))
                    for n in range(NS + 1):
                        if n < NS:
                            for k in range(2):
                                bank_free(pe, CH, BC + 2 * n + k)
                                nc.tensor.matmul(bank(BC + 2 * n + k), s_pick[:, k * NS + n, :], bc[:, :], start=True, stop=True).then_inc(wk_mm, 1)
                        if n >= 1:
                            m = n - 1
                            pe.wait_ge(hc_done, CH * NS + m + 1)
                            if m == 0:
                                pe.wait_ge(y_dve, CH * (DB + 1))
                            for k in range(DB):
                                mm = nc.tensor.matmul(yp[:, k, :], ident[:, :], hc[:, m % 2, k, :], start=(m == 0), stop=(m == NS - 1))
                            mm.then_inc(y_mm, 1)
                    pe.wait_ge(y_dve, (CH + 1) * (DB + 1))
                    project(OUT, s_out, lambda k: u_conv[:, k, :], KT, DB)
                    pe.wait_ge(wk_act, (CH + 1) * READS["act"])
                    project(FROM, s_from, lambda k: o_in[:, k, :], KT, KT)


ATT_IN = ["w_qk", "w_v", "height_rel", "width_rel", "key_hot", "pos_hot", "identity", "group_mean"]
MAM_IN = ["w_to", "b_to", "w_in", "conv_w", "conv_b", "w_x", "w_dt", "b_dt", "a_log", "d_skip", "w_out", "w_from", "b_from",
          "identity", "group_mean", "pick"]


def lay_out(inputs):
    import numpy as np

    a = {k: np.asarray(v) for k, v in inputs.items()}
    w = a["L0_conv_qkv_w"]
    key = np.arange(L)
    key_hot = (key[None, :] % WW == np.arange(WW)[:, None]).astype(np.float32)
    row_hot = (key[None, :L // 2] // WW == np.arange(HH // 2)[:, None]).astype(np.float32)
    channel = np.arange(P)

    def rows(v):
        return np.ascontiguousarray(np.swapaxes(v.reshape(v.shape[0] // P, P, *v.shape[1:]), 0, 1))

    w_x = a["L1_conv_x_proj_w"].T
    w_dt_cols, w_bc_cols = w_x[:, :DR], w_x[:, DR:]
    pick = np.zeros((2, 2 * NS, 2 * NS, P), np.float32)
    pick[:, np.arange(2 * NS), np.arange(2 * NS), :] = 1
    return {
        "x": a["x"].reshape(BATCH, C, L),
        "w_qk": np.ascontiguousarray(w[:2 * C].reshape(2, HEADS, D, C).transpose(3, 1, 0, 2)),
        "w_v": np.ascontiguousarray(w[2 * C:].T.reshape(KT, P, C).transpose(1, 0, 2)),
        "height_rel": np.ascontiguousarray(a["L0_conv_height_rel"].T),
        "width_rel": np.ascontiguousarray(a["L0_conv_width_rel"].T),
        "key_hot": key_hot,
        "pos_hot": np.concatenate([key_hot[:, :L // 2], row_hot, row_hot]),
        "identity": np.eye(P, dtype=np.float32),
        "group_mean": (channel[:, None] // 8 == channel[None, :] // 8).astype(np.float32) / 8,
        "w_to": rows(a["L1_conv_to_seq_w"].T),
        "b_to": rows(a["L1_conv_to_seq_b"]),
        "w_in": rows(a["L1_conv_in_proj_w"].T),
        "conv_w": rows(a["L1_conv_conv_w"]),
        "conv_b": rows(a["L1_conv_conv_b"]),
        "w_x": rows(np.concatenate([w_bc_cols, w_bc_cols, w_dt_cols], axis=1)),
        "w_dt": np.ascontiguousarray(a["L1_conv_dt_proj_w"].T),
        "b_dt": rows(a["L1_conv_dt_proj_b"]),
        "a_log": rows(a["L1_conv_A_log"]),
        "d_skip": rows(a["L1_conv_D"]),
        "w_out": rows(a["L1_conv_out_proj_w"].T),
        "w_from": rows(a["L1_conv_from_seq_w"].T),
        "b_from": rows(a["L1_conv_from_seq_b"]),
        "pick": pick.reshape(4 * NS, 2 * NS, P),
    }


def kernel(**inputs):
    import numpy as np
    from concourse import bacc
    from concourse.bass_utils import run_bass_kernel_spmd

    arrays = lay_out(inputs)
    nc = bacc.Bacc("TRN2", target_bir_lowering=False, num_devices=1)
    dram = {n: nc.dram_tensor(n, v.shape, mybir.dt.from_np(v.dtype), kind="ExternalInput").ap() for n, v in arrays.items()}
    x1 = nc.dram_tensor("x1", [BATCH, C, L], F32).ap()
    out = nc.dram_tensor("out", [BATCH, C, L], F32, kind="ExternalOutput").ap()
    attention_layer(nc, dram["x"], x1, *[dram[n] for n in ATT_IN])
    mamba_layer(nc, x1, out, *[dram[n] for n in MAM_IN])
    r = run_bass_kernel_spmd(nc, [arrays], core_ids=[0])
    return r.results[0]["out"].reshape(BATCH, C, HH, WW)
```

```python
from contextlib import ExitStack

import concourse.bass as bass
from concourse import mybir

F32 = mybir.dt.float32
F32R = mybir.dt.float32r
ALU = mybir.AluOpType
ACT = mybir.ActivationFunctionType
AX = mybir.AxisListType

BATCH, C, HH, WW = 2, 256, 64, 64
L = HH * WW
P = 128
KT = C // P
EPS = 1e-5

HEADS, D = 4, 64
SCALE = float(D) ** -0.5
QB = 512
NB = L // QB
QT = QB // P
NKT = L // P
GK = 2
NG = NKT // GK
NCH = L // 512
REL = 2 * WW - 1
YQ = QB // WW
PREP_UNITS = 28
PREP_ACT, PREP_DVE, BLK_ACT, BLK_POOL = 28, 20, 3, 4

DI, NS, DC, DR = 512, 16, 4, 16
DB = DI // P
T = 512
NC = L // T
GN_DVE = 25


def stand_apart(e, passed):
    e.sem_inc(passed, 1)


def group_norm(nc, role, e, gi, xn, loaded, s, t):
    if role == "vector":
        base = gi * GN_DVE
        e.wait_ge(loaded, 16 * gi + 16)
        for k in range(KT):
            for j in range(L // 512):
                nc.vector.bn_stats(t["st"][:, k, j, :], xn[:, k, j * 512:(j + 1) * 512]).then_inc(s["gn_dve"], 1)
        e.wait_ge(s["gn_dve"], base + 16)
        stand_apart(e, t["passed"])
        for k in range(KT):
            nc.vector.bn_aggr(t["mv"][:, k, :], t["st"][:, k, :, :].rearrange("p a b -> p (a b)")).then_inc(s["gn_dve"], 1)
        e.wait_ge(s["gn_pe"], 2 * gi + 1)
        nc.vector.tensor_copy(t["mg"][:, :, :], t["gps"][:, 0:2 * KT].rearrange("p (k m) -> p k m", k=KT)).then_inc(s["gn_dve"], 1)
        e.wait_ge(s["gn_dve"], base + 19)
        nc.vector.tensor_tensor(t["df"][:, :], t["mv"][:, :, 0], t["mg"][:, :, 0], ALU.subtract).then_inc(s["gn_dve"], 1)
        e.wait_ge(s["gn_dve"], base + 20)
        nc.vector.tensor_tensor(t["sq"][:, :], t["df"][:, :], t["df"][:, :], ALU.mult).then_inc(s["gn_dve"], 1)
        e.wait_ge(s["gn_pe"], 2 * gi + 2)
        nc.vector.scalar_tensor_tensor(out=t["va"][:, :], in0=t["gps"][:, 0:KT], scalar=EPS, in1=t["mg"][:, :, 1],
                                       op0=ALU.add, op1=ALU.add).then_inc(s["gn_dve"], 1)
        e.wait_ge(s["gn_act"], gi + 1)
        nc.vector.reciprocal(t["rs"][:, :], t["sd"][:, :]).then_inc(s["gn_dve"], 1)
        e.wait_ge(s["gn_dve"], base + 23)
        for k in range(KT):
            nc.vector.tensor_scalar(xn[:, k, :], xn[:, k, :], t["mg"][:, k, 0:1], t["rs"][:, k:k + 1],
                                    ALU.subtract, ALU.mult).then_inc(s["gn_dve"], 1)
    elif role == "tensor":
        e.wait_ge(s["gn_dve"], gi * GN_DVE + 18)
        nc.tensor.matmul(t["gps"][:, 0:2 * KT], t["gavg"][:, :], t["mv"][:, :, :].rearrange("p k m -> p (k m)"),
                         start=True, stop=True).then_inc(s["gn_pe"], 1)
        e.wait_ge(s["gn_dve"], gi * GN_DVE + 21)
        nc.tensor.matmul(t["gps"][:, 0:KT], t["gavg"][:, :], t["sq"][:, :], start=True, stop=True).then_inc(s["gn_pe"], 1)
    elif role == "scalar":
        e.wait_ge(s["gn_dve"], gi * GN_DVE + 22)
        nc.scalar.activation(t["sd"][:, :], t["va"][:, :], ACT.Sqrt).then_inc(s["gn_act"], 1)


GN_STATS, GN_ALL = 18, 2 * 25 - 4


def gn_stats(nc, e, b, xn, loaded, s, t):
    e.wait_ge(loaded, 16 * b + 16)
    for k in range(KT):
        for j in range(L // 512):
            nc.vector.bn_stats(t["st"][:, k, j, :], xn[:, k, j * 512:(j + 1) * 512]).then_inc(s["gn_dve"], 1)
    e.wait_ge(s["gn_dve"], b * GN_STATS + 16)
    for k in range(KT):
        nc.vector.bn_aggr(t["mv"][:, k, :], t["st"][:, k, :, :].rearrange("p a b -> p (a b)")).then_inc(s["gn_dve"], 1)


def gn_scale(nc, role, e, b, _, s, t):
    base = BATCH * GN_STATS + 5 * b
    if role == "vector":
        e.wait_ge(s["gn_pe"], 2 * b + 1)
        nc.vector.tensor_copy(t["mg"][:, :, :], t["gps"][:, 0:2 * KT].rearrange("p (k m) -> p k m", k=KT)).then_inc(s["gn_dve"], 1)
        e.wait_ge(s["gn_dve"], base + 1)
        nc.vector.tensor_tensor(t["df"][:, :], t["mv"][:, :, 0], t["mg"][:, :, 0], ALU.subtract).then_inc(s["gn_dve"], 1)
        e.wait_ge(s["gn_dve"], base + 2)
        nc.vector.tensor_tensor(t["sq"][:, :], t["df"][:, :], t["df"][:, :], ALU.mult).then_inc(s["gn_dve"], 1)
        e.wait_ge(s["gn_pe"], 2 * b + 2)
        nc.vector.scalar_tensor_tensor(out=t["va"][:, :], in0=t["gps"][:, 0:KT], scalar=EPS, in1=t["mg"][:, :, 1],
                                       op0=ALU.add, op1=ALU.add).then_inc(s["gn_dve"], 1)
        e.wait_ge(s["gn_act"], b + 1)
        nc.vector.reciprocal(t["rs"][:, :], t["sd"][:, :]).then_inc(s["gn_dve"], 1)
        e.wait_ge(s["gn_dve"], base + 5)
    elif role == "tensor":
        if b:
            e.wait_ge(s["gn_dve"], base)
        else:
            e.wait_ge(s["gn_dve"], BATCH * GN_STATS)
        nc.tensor.matmul(t["gps"][:, 0:2 * KT], t["gavg"][:, :], t["mv"][:, :, :].rearrange("p k m -> p (k m)"),
                         start=True, stop=True).then_inc(s["gn_pe"], 1)
        e.wait_ge(s["gn_dve"], base + 3)
        nc.tensor.matmul(t["gps"][:, 0:KT], t["gavg"][:, :], t["sq"][:, :], start=True, stop=True).then_inc(s["gn_pe"], 1)
    elif role == "scalar":
        e.wait_ge(s["gn_dve"], base + 4)
        nc.scalar.activation(t["sd"][:, :], t["va"][:, :], ACT.Sqrt).then_inc(s["gn_act"], 1)


def gn_tiles(sb, layer):
    return {"st": sb(layer + "_gn_stats", [P, KT, L // 512, 6]), "mv": sb(layer + "_gn_meanvar", [P, KT, 2]),
            "mg": sb(layer + "_gn_group", [P, KT, 2]), "df": sb(layer + "_gn_diff", [P, KT]), "sq": sb(layer + "_gn_square", [P, KT]),
            "va": sb(layer + "_gn_var", [P, KT]), "sd": sb(layer + "_gn_sd", [P, KT]), "rs": sb(layer + "_gn_rstd", [P, KT])}


def attention_layer(nc, x, x1, w_qk, w_v, height_rel, width_rel, key_hot, pos_hot, identity, group_mean):
    with ExitStack() as ctx:
        def sb(name, shape, dt=F32):
            return ctx.enter_context(nc.sbuf_tensor(name, shape, dt))

        def sem(name):
            return ctx.enter_context(nc.semaphore(name))

        xn = sb("a_xn", [P, KT, L])
        k_pos = sb("a_k_pos", [P, L], F32R)
        k_hl = sb("a_k_hl", [P, L], F32R)
        pos = sb("a_pos", [P, L // 2], F32R)
        v_hl = sb("a_v_hl", [P, NKT, P], F32R)
        q_all = sb("a_q", [P, L])
        w_all = sb("a_w", [P, L], F32R)
        m_hi = sb("a_m_hi", [P, 2, QB], F32R)
        m_lo = sb("a_m_lo", [P, 2, QB], F32R)
        m_pos = sb("a_m_pos", [P, 2, 2, QB], F32R)
        q_blk = sb("a_q_blk", [D, QB])
        probs = sb("a_probs", [P, 2, GK, QB])
        p_hi = sb("a_p_hi", [P, 4, GK, QB], F32R)
        p_lo = sb("a_p_lo", [P, 4, GK, QB], F32R)
        p_sum = sb("a_p_sum", [P, 2, GK, QB])
        w_head = sb("a_w_head", [P, KT, 2, 2, D])
        w_val = sb("a_w_val", [P, KT, C])
        hrel = sb("a_hrel", [D, REL + 1])
        wrel = sb("a_wrel", [D, REL + 1])
        ident = sb("a_ident", [P, P])
        gavg = sb("a_gavg", [P, P])
        col_max = sb("a_col_max", [P, QT, HH])
        row_sum = sb("a_row_sum", [P, QT, HH])
        q_max = sb("a_q_max", [P, QT])
        r_less = sb("a_r_less", [P, QT, 3 * D])
        rh = sb("a_rh", [P, QT, 66])
        ones = sb("a_ones", [P, D])
        weighed = sb("a_weighed", [D, QB])
        rec = sb("a_rec", [D, QB])
        x_res = sb("a_x_res", [D, 2, QB])
        t = gn_tiles(sb, "a")
        t["gavg"] = gavg

        sc = ctx.enter_context(nc.psum_tensor("a_scores", [P, 2, GK, QB], F32))
        mx = ctx.enter_context(nc.psum_tensor("a_mx", [P, 2, 512], F32))
        oa = ctx.enter_context(nc.psum_tensor("a_oa", [P, QB], F32))
        mi = ctx.enter_context(nc.psum_tensor("a_mi", [P, 512], F32))
        t["gps"] = mi
        rh_ps = mx[:, 0, 0:QT * 66].rearrange("p (t r) -> p t r", t=QT)

        s = {n: sem("a_" + n) for n in ("gn_dve", "gn_pe", "gn_act")}
        const_in, x_in, wh_in = (sem("a_" + n) for n in ("const_in", "x_in", "wh_in"))
        res_in, x1_out = ([sem(f"a_{n}{k}") for k in range(2)] for n in ("res_in", "x1_out"))
        ones_set, hot_in = sem("a_ones_set"), sem("a_hot_in")
        passed = t["passed"] = sem("a_passed")
        proj_mm, prep_act, prep_dve, prep_pool = (sem("a_" + n) for n in ("proj_mm", "prep_act", "prep_dve", "prep_pool"))
        blk_act, rh_dve = sem("a_blk_act"), sem("a_rh_dve")
        blk_pool, mx_mm, mx_red, rh_mm, sum_dve, max_dve, rp_dve, tr_mm, hi_act, lo_dve = (
            sem("a_" + n) for n in ("blk_pool", "mx_mm", "mx_red", "rh_mm", "sum_dve", "max_dve", "rp_dve", "tr_mm",
                                    "hi_act", "lo_dve"))
        score_mm, exp_act, lo_p, sum_pool, pv_mm, half_dve, oa_read, total_mm, rec_dve, div_pool, out_pool = (
            sem("a_" + n) for n in ("score_mm", "exp_act", "lo_p", "sum_pool", "pv_mm", "half_dve", "oa_read", "total_mm",
                                    "rec_dve", "div_pool", "out_pool"))
        EXP0, LO0, SUM0 = 4, 2, 2

        def exp_count(B, g, which):
            return EXP0 + 2 * (B * NG + g) + which

        MAX_AT = {g: list(range(3 * (g - 2), min(3 * (g - 2) + 3, QT * NCH))) for g in range(2, 13)}
        N_CONST = 5


        def unit_bank(u):
            return sc[:, (u % 4) // 2, u % 2, :]

        def main_blocks(e, body):
            body(0, 0, False, True)
            body(0, 1, True, True)
            with e.Fori(1, NB // 2 - 1) as ii:
                body(ii, 0, True, True)
                body(ii, 1, True, True)
            body(NB // 2 - 1, 0, True, True)
            body(NB // 2 - 1, 1, True, False)

        block = ctx.enter_context(nc.Block())

        @block.sync
        def _(sp):
            for dst, src in ((w_val[:, :, :], w_v), (hrel[:, 0:REL], height_rel), (wrel[:, 0:REL], width_rel),
                             (ident[:, :], identity), (gavg[:, :], group_mean)):
                sp.dma_start(dst, src).then_inc(const_in, 16)
            with sp.Fori(0, BATCH) as b:
                sp.wait_ge(proj_mm, b * (HEADS * PREP_UNITS))
                sp.dma_start(xn[:, :, :], x[bass.ds(b, 1), :, :].rearrange("o (k p) l -> (o p) k l", p=P)).then_inc(x_in, 16)
                with sp.Fori(0, HEADS) as h:
                    H = b * HEADS + h
                    sp.wait_ge(proj_mm, H * PREP_UNITS)
                    for k in range(KT):
                        for dup in range(2):
                            sp.dma_start(w_head[:, k, :, dup, :], w_qk[k * P:(k + 1) * P, bass.ds(h, 1), :, :]
                                         .rearrange("p o r d -> p (o r) d")).then_inc(wh_in, 16)
                    for i in range(NB):
                        sp.wait_ge(x1_out[i % 2], H * (8 * NB) + 16 * (i // 2))
                        sp.dma_start(x_res[:, i % 2, :], x[bass.ds(b, 1), bass.ds(h * D, D), i * QB:(i + 1) * QB]
                                     .rearrange("o c l -> (o c) l")).then_inc(res_in[i % 2], 16)
            for k in range(2):
                sp.wait_ge(x1_out[k], 8 * BATCH * HEADS * NB)

        @block.gpsimd
        def _(pool):
            pool.dma_start(pos[:, :], pos_hot).then_inc(hot_in, 16)
            pool.dma_start(k_pos[D:P, :], key_hot).then_inc(hot_in, 16)
            nc.gpsimd.memset(ones[:, :], 1.0).then_inc(ones_set, 1)
            nc.gpsimd.memset(r_less[:, :, 0:D], 0.0).then_inc(ones_set, 1)
            pool.sem_inc(sum_pool, SUM0)

            def block_operands(H, i, sl, sums_done):
                blk = bass.ds(i * QB, QB)
                B = H * NB + i
                cp = nc.gpsimd.tensor_copy
                pool.wait_ge(sum_pool, SUM0 + sums_done)
                stand_apart(pool, passed)
                cp(m_hi[D:P, sl, :], w_all[D:P, blk]).then_inc(blk_pool, 1)
                for half in range(2):
                    cp(m_pos[0:D, sl, half, :], w_all[0:D, blk]).then_inc(blk_pool, 1)
                pool.wait_ge(blk_act, B * BLK_ACT + BLK_ACT)
                stand_apart(pool, passed)
                nc.gpsimd.tensor_tensor(m_lo[0:D, sl, :], q_all[0:D, blk], m_hi[0:D, sl, :], ALU.subtract).then_inc(blk_pool, 1)
                pool.wait_ge(blk_pool, B * BLK_POOL + BLK_POOL)

            with pool.Fori(0, BATCH) as b:
                with pool.Fori(0, HEADS) as h:
                    H = b * HEADS + h
                    for c in range(NCH):
                        pool.wait_ge(prep_act, H * PREP_ACT + c + 1)
                        stand_apart(pool, passed)
                        nc.gpsimd.tensor_copy(k_pos[0:D, c * 512:(c + 1) * 512], k_hl[0:D, c * 512:(c + 1) * 512]).then_inc(prep_pool, 1)
                    pool.wait_ge(prep_act, H * PREP_ACT + PREP_ACT)
                    pool.wait_ge(prep_dve, H * PREP_DVE + PREP_DVE)
                    block_operands(H, 0, 0, H * NB * NG)

                    def finish(done, i, sl):
                        pool.wait_ge(rec_dve, QT * done)
                        nc.gpsimd.tensor_tensor(weighed[:, :], weighed[:, :], rec[:, :], ALU.mult).then_inc(div_pool, 1)
                        pool.wait_ge(div_pool, done)
                        pool.wait_ge(res_in[sl], H * (8 * NB) + 8 * (i - sl) + 16)
                        nc.gpsimd.tensor_tensor(x_res[:, sl, :], weighed[:, :], x_res[:, sl, :], ALU.add).then_inc(out_pool, 1)
                        pool.wait_ge(out_pool, done)
                        pool.dma_start(x1[bass.ds(b, 1), bass.ds(h * D, D), bass.ds(i * QB, QB)].rearrange("o c l -> (o c) l"),
                                       x_res[:, sl, :]).then_inc(x1_out[sl], 16)

                    def body(ii, sl, prev, nxt):
                        i = 2 * ii + sl
                        B = H * NB + i
                        if nxt:
                            if prev:
                                pool.wait_ge(pv_mm, B * NG - 2)
                            block_operands(H, i + 1, 1 - sl, B * NG)
                        for g in range(NG):
                            pool.wait_ge(exp_act, exp_count(B, g, 1))
                            if g == 0:
                                if prev:
                                    pool.wait_ge(total_mm, B - 1)
                                stand_apart(pool, passed)
                                nc.gpsimd.tensor_copy(p_sum[:, sl, :, :], probs[:, g % 2, :, :]).then_inc(sum_pool, 1)
                            else:
                                pool.wait_ge(sum_pool, SUM0 + B * NG + g)
                                nc.gpsimd.tensor_tensor(p_sum[:, sl, :, :], p_sum[:, sl, :, :], probs[:, g % 2, :, :],
                                                        ALU.add).then_inc(sum_pool, 1)
                            if g == 8 and prev:
                                finish(B, i - 1, 1 - sl)
                        if not nxt:
                            finish(B + 1, i, sl)

                    main_blocks(pool, body)

        @block.scalar
        def _(act):
            act.sem_inc(exp_act, EXP0)

            def block_operands(H, i, sl):
                blk = bass.ds(i * QB, QB)
                act.wait_ge(rh_mm, H * NB + i)
                nc.scalar.activation(q_blk[:, :], q_all[0:D, blk], ACT.Copy).then_inc(blk_act, 1)
                nc.scalar.activation(m_hi[0:D, sl, :], q_all[0:D, blk], ACT.Copy).then_inc(blk_act, 1)
                nc.scalar.activation(m_lo[D:P, sl, :], q_all[D:P, blk], ACT.Copy).then_inc(blk_act, 1)

            with act.Fori(0, BATCH) as b:
                group_norm(nc, "scalar", act, b, xn, x_in, s, t)
                with act.Fori(0, HEADS) as h:
                    H = b * HEADS + h
                    for u in range(8):
                        act.wait_ge(proj_mm, H * PREP_UNITS + u + 1)
                        nc.scalar.activation(k_hl[:, u * 512:(u + 1) * 512], unit_bank(u), ACT.Copy, scale=SCALE).then_inc(prep_act, 1)
                    for u in range(8, 16):
                        act.wait_ge(proj_mm, H * PREP_UNITS + u + 1)
                        nc.scalar.activation(q_all[:, (u - 8) * 512:(u - 7) * 512], unit_bank(u), ACT.Copy).then_inc(prep_act, 1)
                    for u in range(16, 20):
                        act.wait_ge(proj_mm, H * PREP_UNITS + u + 1)
                        nc.scalar.activation(v_hl[:, 8 * (u - 16):8 * (u - 15), 0:D],
                                             unit_bank(u).rearrange("p (t d) -> p t d", t=8), ACT.Copy).then_inc(prep_act, 1)
                    block_operands(H, 0, 0)
                    for u in range(20, 28):
                        act.wait_ge(proj_mm, H * PREP_UNITS + u + 1)
                        nc.scalar.activation(w_all[:, :].rearrange("p (y x) -> p x y", x=WW)[:, 8 * (u - 20):8 * (u - 19), :],
                                             unit_bank(u).rearrange("p (x y) -> p x y", x=8), ACT.Copy).then_inc(prep_act, 1)

                    def r_hi(B, sl):
                        act.wait_ge(tr_mm, B + 1)
                        nc.scalar.activation(m_pos[D:P, sl, :, :], mx[D:P, :, :], ACT.Copy).then_inc(hi_act, 1)

                    r_hi(H * NB, 0)

                    def body(ii, sl, prev, nxt):
                        i = 2 * ii + sl
                        B = H * NB + i
                        for g in range(NG):
                            act.wait_ge(score_mm, B * NG + g + 1)
                            act.wait_ge(lo_p, LO0 + B * NG + g - 1)
                            act.wait_ge(sum_pool, SUM0 + B * NG + g - 1)
                            nc.scalar.activation(probs[:, g % 2, :, :], sc[:, g % 2, :, :], ACT.Exp).then_inc(exp_act, 1)
                            nc.scalar.activation(p_hi[:, g % 4, :, :], sc[:, g % 2, :, :], ACT.Exp).then_inc(exp_act, 1)
                            if g == 0 and nxt:
                                block_operands(H, i + 1, 1 - sl)
                            if g == 14 and nxt:
                                r_hi(B + 1, 1 - sl)

                    main_blocks(act, body)

        @block.vector
        def _(dve):
            dve.sem_inc(lo_p, LO0)
            with dve.Fori(0, BATCH) as b:
                group_norm(nc, "vector", dve, b, xn, x_in, s, t)
                with dve.Fori(0, HEADS) as h:
                    H = b * HEADS + h
                    for u in range(8):
                        dve.wait_ge(prep_act, H * PREP_ACT + u + 1)
                        sl_ = slice(u * 512, (u + 1) * 512)
                        nc.vector.scalar_tensor_tensor(out=k_hl[D:P, sl_], in0=unit_bank(u)[D:P, :], scalar=SCALE,
                                                       in1=k_hl[D:P, sl_], op0=ALU.mult, op1=ALU.subtract).then_inc(prep_dve, 1)
                    for u in range(16, 20):
                        dve.wait_ge(prep_act, H * PREP_ACT + u + 1)
                        v8 = v_hl[:, 8 * (u - 16):8 * (u - 15), :]
                        nc.vector.tensor_tensor(v8[:, :, D:P], unit_bank(u).rearrange("p (t d) -> p t d", t=8), v8[:, :, 0:D],
                                                ALU.subtract).then_inc(prep_dve, 1)
                    for u in range(20, 28):
                        dve.wait_ge(prep_act, H * PREP_ACT + u + 1)
                        w_ap = w_all[0:D, :].rearrange("p (y x) -> p x y", x=WW)[:, 8 * (u - 20):8 * (u - 19), :]
                        nc.vector.tensor_tensor(w_ap, unit_bank(u)[0:D, :].rearrange("p (x y) -> p x y", x=8), w_ap,
                                                ALU.subtract).then_inc(prep_dve, 1)

                    def height_copy(B):
                        dve.wait_ge(rh_mm, B + 1)
                        nc.vector.tensor_copy(rh[:, :, 0:HH + 1], rh_ps[:, :, 0:HH + 1]).then_inc(rh_dve, 1)

                    def column_max(B, ks):
                        for k in ks:
                            qt, c = divmod(k, NCH)
                            dve.wait_ge(mx_mm, B * (QT * NCH) + k + 1)
                            nc.vector.tensor_reduce(col_max[:, qt, c * 8:(c + 1) * 8],
                                                    mx[:, k % 2, :].rearrange("p (y x) -> p y x", x=WW), AX.X, ALU.max).then_inc(mx_red, 1)

                    def less_max(B):
                        dve.wait_ge(rh_dve, B + 1)
                        dve.wait_ge(mx_red, B * (QT * NCH) + QT * NCH)
                        for half in range(2):
                            r = slice(half * D, half * D + D)
                            nc.vector.tensor_tensor(row_sum[r, :, :], rh[r, :, 1 - half:1 - half + HH], col_max[r, :, :], ALU.add).then_inc(sum_dve, 1)
                        dve.wait_ge(sum_dve, 2 * B + 2)
                        nc.vector.tensor_reduce(q_max[:, :], row_sum[:, :, :], AX.X, ALU.max).then_inc(max_dve, 1)
                        dve.wait_ge(max_dve, B + 1)
                        for half in range(2):
                            r = slice(half * D, half * D + D)
                            for kh in range(2):
                                c0 = 1 - half + kh * 32
                                nc.vector.tensor_tensor(r_less[r, :, D + kh * D:2 * D + kh * D].rearrange("p t (a y) -> p t a y", a=2),
                                                        rh[r, :, c0:c0 + 32].unsqueeze(2).to_broadcast([D, QT, 2, 32]),
                                                        q_max[r, :].unsqueeze(2).unsqueeze(3).to_broadcast([D, QT, 2, 32]),
                                                        ALU.subtract).then_inc(rp_dve, 1)

                    def r_lo(B, sl):
                        dve.wait_ge(hi_act, B + 1)
                        nc.vector.tensor_tensor(m_pos[96:P, sl, :, :], mx[96:P, :, :], m_pos[96:P, sl, :, :], ALU.subtract).then_inc(lo_dve, 1)

                    def low_probs(B, g):
                        dve.wait_ge(exp_act, exp_count(B, g, 2))
                        nc.vector.tensor_tensor(p_lo[:, g % 4, :, :], probs[:, g % 2, :, :], p_hi[:, g % 4, :, :],
                                                ALU.subtract).then_inc(lo_p, 1)

                    def take_weighed(done):
                        dve.wait_ge(pv_mm, done * NG)
                        dve.wait_ge(div_pool, done - 1)
                        nc.vector.tensor_copy(weighed[:, :], oa[D:P, :]).then_inc(half_dve, 1)
                        dve.wait_ge(half_dve, done)
                        nc.vector.tensor_tensor(weighed[:, :], oa[0:D, :], weighed[:, :], ALU.add).then_inc(oa_read, 1)

                    def take_total(done, part):
                        if part == 0:
                            dve.wait_ge(total_mm, done)
                        q4 = slice(part * P, (part + 1) * P)
                        nc.vector.reciprocal(rec[:, q4], mi[0:D, q4]).then_inc(rec_dve, 1)

                    height_copy(H * NB)
                    column_max(H * NB, range(QT * NCH))
                    less_max(H * NB)
                    r_lo(H * NB, 0)

                    def body(ii, sl, prev, nxt):
                        i = 2 * ii + sl
                        B = H * NB + i
                        for g in range(NG):
                            if nxt and g == 2:
                                height_copy(B + 1)
                            if nxt:
                                column_max(B + 1, MAX_AT.get(g, []))
                            if nxt and g == 13:
                                less_max(B + 1)
                            if g >= 1:
                                low_probs(B, g - 1)
                            elif prev:
                                low_probs(B - 1, NG - 1)
                            if prev and g == 1:
                                take_weighed(B)
                            if prev and 4 <= g < 4 + QT:
                                take_total(B, g - 4)
                            if nxt and g == 15:
                                r_lo(B + 1, 1 - sl)
                        if not nxt:
                            low_probs(B, NG - 1)
                            take_weighed(B + 1)
                            for part in range(QT):
                                take_total(B + 1, part)

                    main_blocks(dve, body)

        @block.tensor
        def _(pe):
            pe.wait_ge(const_in, 16 * N_CONST)
            pe.wait_ge(hot_in, 32)
            pe.wait_ge(ones_set, 2)
            with pe.Fori(0, BATCH) as b:
                group_norm(nc, "tensor", pe, b, xn, x_in, s, t)
                pe.wait_ge(s["gn_dve"], b * GN_DVE + GN_DVE)
                stand_apart(pe, passed)
                with pe.Fori(0, HEADS) as h:
                    H = b * HEADS + h
                    pe.wait_ge(wh_in, H * 64 + 64)
                    pe.wait_ge(exp_act, exp_count(H * NB, -1, 2))

                    def bank_free(u):
                        v = u - 4
                        if v < 0:
                            return
                        if v < 8:
                            pe.wait_ge(prep_dve, H * PREP_DVE + v + 1)
                        elif v < 16:
                            pe.wait_ge(prep_act, H * PREP_ACT + v + 1)
                        else:
                            pe.wait_ge(prep_dve, H * PREP_DVE + v - 8 + 1)

                    for u in range(16):
                        bank_free(u)
                        role, c = (1, u) if u < 8 else (0, u - 8)
                        for k in range(KT):
                            mm = nc.tensor.matmul(unit_bank(u), w_head[:, k, role, :, :].rearrange("p a d -> p (a d)"),
                                                  xn[:, k, c * 512:(c + 1) * 512], start=(k == 0), stop=(k == KT - 1))
                        mm.then_inc(proj_mm, 1)
                    for u in range(16, 20):
                        bank_free(u)
                        for j in range(8):
                            tok = slice(((u - 16) * 8 + j) * P, ((u - 16) * 8 + j + 1) * P)
                            for k in range(KT):
                                mm = nc.tensor.matmul(unit_bank(u)[:, j * D:(j + 1) * D], xn[:, k, tok],
                                                      w_val[:, k, bass.ds(h * D, D)], start=(k == 0), stop=(k == KT - 1))
                        mm.then_inc(proj_mm, 1)
                    pe.wait_ge(prep_act, H * PREP_ACT + 16)
                    for u in range(20, 28):
                        bank_free(u)
                        stand_apart(pe, passed)
                        for j in range(8):
                            xq = (u - 20) * 8 + j
                            for half in range(2):
                                mm = nc.tensor.matmul(unit_bank(u)[half * D:half * D + D, j * HH:(j + 1) * HH],
                                                      wrel[:, WW - 1 - xq:2 * WW - 1 - xq],
                                                      q_all[0:D, :].rearrange("p (y x) -> p x y", x=WW)[:, xq, :],
                                                      start=True, stop=True)
                        mm.then_inc(proj_mm, 1)

                    def height_logits(B, i):
                        pe.wait_ge(blk_act, B * BLK_ACT + BLK_ACT)
                        pe.wait_ge(lo_dve, B)
                        for qt in range(QT):
                            win = hrel[:, bass.ds(WW - 2 - 2 * qt - i * YQ, HH + 1)]
                            mm = nc.tensor.matmul(rh_ps[:, qt, 0:HH + 1], q_blk[:, qt * P:(qt + 1) * P], win, start=True, stop=True)
                        mm.then_inc(rh_mm, 1)

                    def max_scores(B, sl, k):
                        qt, c = divmod(k, NCH)
                        if k == 0:
                            pe.wait_ge(blk_pool, B * BLK_POOL + BLK_POOL)
                            pe.wait_ge(rh_dve, B + 1)
                        elif k >= 2:
                            pe.wait_ge(mx_red, B * (QT * NCH) + k - 1)
                        nc.tensor.matmul(mx[:, k % 2, :], m_hi[:, sl, qt * P:(qt + 1) * P], k_pos[:, c * 512:(c + 1) * 512],
                                         start=True, stop=True).then_inc(mx_mm, 1)

                    def turn(B):
                        pe.wait_ge(rp_dve, 4 * B + 4)
                        for half in range(2):
                            for qt in range(QT):
                                mm = nc.tensor.transpose(mx[:, half, qt * P:(qt + 1) * P], r_less[:, qt, half * D:half * D + P], ident[:, :])
                        mm.then_inc(tr_mm, 1)

                    def scores(B, g, j, sl):
                        kt = g * GK + j
                        keys = slice(kt * P, (kt + 1) * P)
                        half, kp = divmod(kt, NKT // 2)
                        if j == 0:
                            pe.wait_ge(exp_act, exp_count(B, g - 2, 2))
                        nc.tensor.matmul(sc[:, g % 2, j, :], k_pos[:, keys], m_hi[:, sl, :], start=True, stop=False)
                        nc.tensor.matmul(sc[:, g % 2, j, :], k_hl[:, keys], m_lo[:, sl, :], start=False, stop=False)
                        mm = nc.tensor.matmul(sc[:, g % 2, j, :], pos[:, kp * P:(kp + 1) * P], m_pos[:, sl, half, :],
                                              start=False, stop=True)
                        if j == GK - 1:
                            mm.then_inc(score_mm, 1)

                    def weigh(B, g, part):
                        if part == 0:
                            pe.wait_ge(exp_act, exp_count(B, g, 2))
                            if g == 0:
                                pe.wait_ge(oa_read, B)
                        else:
                            pe.wait_ge(lo_p, LO0 + B * NG + g + 1)
                        for j in range(GK):
                            kt = g * GK + j
                            mm = nc.tensor.matmul(oa[:, :], v_hl[:, kt, :], (p_hi, p_lo)[part][:, g % 4, j, :],
                                                  start=(kt == 0 and part == 0), stop=(kt == NKT - 1 and part == 1))
                        if part == 1:
                            mm.then_inc(pv_mm, 1)

                    def totals(done, sl):
                        pe.wait_ge(sum_pool, SUM0 + done * NG)
                        pe.wait_ge(rec_dve, QT * (done - 1))
                        for j in range(GK):
                            mm = nc.tensor.matmul(mi[0:D, :], ones[:, :], p_sum[:, sl, j, :], start=(j == 0), stop=(j == GK - 1))
                        mm.then_inc(total_mm, 1)

                    height_logits(H * NB, 0)
                    pe.wait_ge(prep_pool, H * NCH + NCH)
                    for k in range(QT * NCH):
                        max_scores(H * NB, 0, k)
                    turn(H * NB)
                    pe.wait_ge(prep_dve, H * PREP_DVE + PREP_DVE)
                    stand_apart(pe, passed)

                    def body(ii, sl, prev, nxt):
                        i = 2 * ii + sl
                        B = H * NB + i

                        pe.wait_ge(lo_dve, B + 1)
                        for g in range(NG):
                            ks = list(MAX_AT.get(g, [])) if nxt else []

                            def one_max():
                                if ks:
                                    max_scores(B + 1, 1 - sl, ks.pop(0))

                            back = (B, g - 2) if g >= 2 else (B - 1, NG - 2 + g) if prev else None
                            scores(B, g, 0, sl)
                            one_max()
                            scores(B, g, 1, sl)
                            if nxt and g == 1:
                                height_logits(B + 1, i + 1)
                            if back:
                                weigh(*back, 0)
                            one_max()
                            if back:
                                weigh(*back, 1)
                            one_max()
                            if prev and g == 3:
                                totals(B, 1 - sl)
                            if nxt and g == 14:
                                turn(B + 1)
                        if not nxt:
                            for g in (NG - 2, NG - 1):
                                weigh(B, g, 0)
                                weigh(B, g, 1)
                            totals(B + 1, sl)

                    main_blocks(pe, body)


def mamba_layer(nc, x1, out, w_to, b_to, w_in, conv_w, conv_b, w_x, w_dt, b_dt, a_log, d_skip, w_out, w_from, b_from,
                identity, group_mean, pick):
    with ExitStack() as ctx:
        def sb(name, shape, dt=F32):
            return ctx.enter_context(nc.sbuf_tensor(name, shape, dt))

        def sem(name):
            return ctx.enter_context(nc.semaphore(name))

        x_in_t = sb("m_x_in", [P, KT, T])
        x_res = sb("m_x_res", [P, KT, T])
        seq = sb("m_seq", [P, KT, T])
        u_raw = sb("m_u_raw", [P, DB, DC - 1 + T])
        u_conv = sb("m_u_conv", [P, DB, T])
        u_act = sb("m_u_act", [P, 2, DB, T])
        z_act = sb("m_z_act", [P, 2, DB, T])
        relu_v = sb("m_relu_v", [P, DB, T])
        e_abs = sb("m_e_abs", [P, DB, T])
        delta = sb("m_delta", [P, DB, T])
        du = sb("m_du", [P, DB, T])
        y = sb("m_y", [P, DB, T])
        bc = sb("m_bc", [2 * 2 * NS, 2, T], F32R)
        dt_low = sb("m_dt_low", [5 * NS, T])
        bc_all = sb("m_bc_all", [P, 2, 2, T])
        d_a = sb("m_d_a", [P, 2, DB, T])
        RING = 4
        ring = sb("m_ring", [P, RING, DB, T])
        state = sb("m_state", [P, DB, NS])
        o_in = sb("m_o_in", [P, KT, T])
        s_to, s_in = sb("m_w_to", [P, KT, C]), sb("m_w_in", [P, KT, 2 * DI])
        s_x, s_dt = sb("m_w_x", [P, DB, 5 * NS]), sb("m_w_dt", [5 * NS, DI])
        s_out, s_from = sb("m_w_out", [P, DB, C]), sb("m_w_from", [P, KT, C])
        s_bto, s_bfrom = sb("m_b_to", [P, KT]), sb("m_b_from", [P, KT])
        s_cw, s_cb, s_bdt, s_d = sb("m_conv_w", [P, DB, DC]), sb("m_conv_b", [P, DB]), sb("m_b_dt", [P, DB]), sb("m_d", [P, DB])
        a_exp, a_neg = sb("m_a_exp", [P, DB, NS]), sb("m_a_neg", [P, DB, NS])
        ident, gavg = sb("m_ident", [P, P]), sb("m_gavg", [P, P])
        s_pick = sb("m_pick", [2 * 2 * NS, 2 * NS, P], F32R)
        tiles = [gn_tiles(sb, f"m{b}") for b in range(BATCH)]
        log_e, low_e = y, u_conv
        xn_all = ring[:, :, :, :].rearrange("p r k t -> p (r k t)").rearrange("p (k l) -> p k l", k=KT)

        yp = ctx.enter_context(nc.psum_tensor("m_yp", [P, DB, T], F32))
        wk = ctx.enter_context(nc.psum_tensor("m_wk", [P, 4, T], F32))

        s = {n: sem("m_" + n) for n in ("gn_dve", "gn_pe", "gn_act")}
        passed = sem("m_passed")
        for t in tiles:
            t["gavg"], t["gps"], t["passed"] = gavg, wk[:, 3, :], passed
        const_in, hot_in, all_in, xc_in, res_in, out_out = (
            sem("m_" + n) for n in ("const_in", "hot_in", "all_in", "xc_in", "res_in", "out_out"))
        wk_mm, wk_act, wk_dve = sem("m_wk_mm"), sem("m_wk_act"), sem("m_wk_dve")
        x_norm, halo, conv, act_u, act_z, dt_act = (sem("m_" + n) for n in ("x_norm", "halo", "conv", "act_u", "act_z", "dt_act"))
        v_act, e_act, log_act, one_dve, low_pool, sum_dve, delta_dve, du_dve = (
            sem("m_" + n) for n in ("v_act", "e_act", "log_act", "one_dve", "low_pool", "sum_dve", "delta_dve", "du_dve"))
        a_act, a_dve, state0 = sem("m_a_act"), sem("m_a_dve"), sem("m_state0")
        da_act, dbu, scan, st_dve, hc_done, y_mm, yd_dve, y_pool = (
            sem("m_" + n) for n in ("da_act", "dbu", "scan", "st_dve", "hc_done", "y_mm", "yd_dve", "y_pool"))
        NCHUNK = BATCH * NC

        FRONT = {1: ["SEQ0", "SEQ1"], 4: ["U0", "U1"], 5: ["U2", "U3"], 6: ["Z0", "Z1"], 7: ["Z2", "Z3"], 10: ["XD"],
                 11: ["DT0", "DT1", "DT2", "DT3"]}
        POST = {2: ["OUT0", "OUT1"], 3: ["FROM0", "FROM1"]}

        def order(front, post, states, first_bc):
            units = []
            for n in range(NS):
                if states and n + 1 < NS + (1 if front else 0):
                    units += [f"B{(n + 1) % NS}", f"C{(n + 1) % NS}"]
                units += (FRONT.get(n, []) if front else []) + (POST.get(n, []) if post else [])
            return units + (["B0", "C0"] if first_bc else [])

        ORDER = {"pro": order(True, False, False, True), "first": order(True, False, True, False),
                 "mid": order(True, True, True, False), "last": order(False, True, True, False),
                 "epi": order(False, True, False, False)}

        def scalar_holds(name):
            return name[:2] != "SE" and name[:2] != "FR"

        def vector_holds(name):
            return name[:2] in ("SE", "FR", "XD")

        class BankCount:

            def __init__(self, kind, CH):
                self.kind, self.CH = kind, CH

            def before(self, counted):
                def n(kind):
                    return sum(counted(x) for x in ORDER[kind])
                if self.kind == "pro":
                    return 0
                if self.kind == "first":
                    return n("pro")
                if self.kind == "epi":
                    return n("pro") + n("first") + (NCHUNK - 2) * n("mid") + n("last")
                return n("pro") + n("first") + (self.CH - 1) * n("mid")

            def upto(self, name, counted):
                units = ORDER[self.kind]
                return self.before(counted) + sum(counted(x) for x in units[:units.index(name) + 1])

            def mm(self, name):
                return self.upto(name, lambda x: True)

            def act(self, name):
                return self.upto(name, scalar_holds)

            def dve(self, name):
                return self.upto(name, vector_holds)

            def bank(self, name):
                return wk[:, ORDER[self.kind].index(name) % 4, :]

        def at_least(e, sem_, value):
            if isinstance(value, int) and value <= 0:
                return
            e.wait_ge(sem_, value)

        def chunks(e, body):
            last = NC // 2 - 1
            for b in range(BATCH):
                for q in range(2):
                    body("first" if b == 0 and q == 0 else "mid", b, q, b * NC + q, q)
                with e.Fori(1, last) as cc:
                    for q in range(2):
                        body("mid", b, 2 * cc + q, 2 * cc + (b * NC + q), q)
                for q in range(2):
                    c = 2 * last + q
                    body("last" if b == BATCH - 1 and q == 1 else "mid", b, c, b * NC + c, q)

        def chunk_of(tensor, b, c, off):
            if isinstance(c, int):
                b, c = divmod(b * NC + c + off, NC)
                return tensor[b, :, c * T:(c + 1) * T].rearrange("(k p) l -> p k l", p=P)
            return tensor[b, :, bass.ds((c + off) * T, T)].rearrange("(k p) l -> p k l", p=P)

        block = ctx.enter_context(nc.Block())

        consts = [(s_to, w_to), (s_in, w_in), (s_x, w_x), (s_out, w_out), (s_from, w_from), (s_bto, b_to), (s_bfrom, b_from),
                  (s_cw, conv_w), (s_cb, conv_b), (s_bdt, b_dt), (s_d, d_skip), (a_exp, a_log), (ident, identity), (gavg, group_mean)]

        @block.sync
        def _(sp):
            sp.dma_start(xn_all, x1[0, :, :].rearrange("(k p) l -> p k l", p=P)).then_inc(all_in, 16)
            for dst, src in consts:
                sp.dma_start(dst[tuple(slice(None) for _ in dst.shape)], src).then_inc(const_in, 16)
            sp.dma_start(s_dt[4 * NS:5 * NS, :], w_dt).then_inc(const_in, 16)
            sp.dma_start(x_in_t[:, :, :], chunk_of(x1, 0, 0, 0)).then_inc(xc_in, 16)
            sp.dma_start(x_res[:, :, :], chunk_of(x1, 0, 0, 0)).then_inc(res_in, 16)
            for b in range(1, BATCH):
                sp.wait_ge(s["gn_dve"], (b - 1) * GN_STATS + 16)
                sp.dma_start(xn_all, x1[b, :, :].rearrange("(k p) l -> p k l", p=P)).then_inc(all_in, 16)
            sp.wait_ge(wk_mm, BankCount("pro", 0).mm("SEQ1"))
            sp.dma_start(x_in_t[:, :, :], chunk_of(x1, 0, 0, 1)).then_inc(xc_in, 16)

            def body(kind, b, c, CH, q):
                at = BankCount(kind, CH)
                if kind != "last" and not (isinstance(CH, int) and CH + 2 >= NCHUNK):
                    sp.wait_ge(wk_mm, at.mm("SEQ1"))
                    sp.dma_start(x_in_t[:, :, :], chunk_of(x1, b, c, 2)).then_inc(xc_in, 16)
                if kind != "first":
                    sp.wait_ge(wk_dve, at.dve("FROM1"))
                    sp.dma_start(chunk_of(out, b, c, -1), x_res[:, :, :]).then_inc(out_out, 16)
                    sp.wait_ge(out_out, CH * 16)
                    sp.dma_start(x_res[:, :, :], chunk_of(x1, b, c, 0)).then_inc(res_in, 16)

            chunks(sp, body)
            sp.wait_ge(wk_dve, BankCount("epi", NCHUNK).dve("FROM1"))
            sp.dma_start(chunk_of(out, BATCH - 1, NC - 1, 0), x_res[:, :, :]).then_inc(out_out, 16)
            sp.wait_ge(out_out, 16 * NCHUNK)

        @block.gpsimd
        def _(pool):
            pool.dma_start(s_pick[:, :, :], pick).then_inc(hot_in, 16)

            def low_part(CH):
                pool.wait_ge(one_dve, CH + 1)
                nc.gpsimd.tensor_tensor(low_e[:, :, :], low_e[:, :, :], e_abs[:, :, :], ALU.subtract).then_inc(low_pool, 1)

            def gate(CH, q):
                pool.wait_ge(yd_dve, (CH + 1) * DB)
                nc.gpsimd.tensor_tensor(y[:, :, :], y[:, :, :], z_act[:, q, :, :], ALU.mult).then_inc(y_pool, 1)

            low_part(0)

            def body(kind, b, c, CH, q):
                at = BankCount(kind, CH)
                pool.wait_ge(du_dve, CH + 1)
                for n in range(NS):
                    if n == 0:
                        b_ready = BankCount("pro", 0).act("B0") if kind == "first" else at.before(scalar_holds) - 1
                    else:
                        b_ready = at.act(f"B{n}")
                    pool.wait_ge(wk_act, b_ready)
                    at_least(pool, y_mm, CH * NS + n - (RING - 1))
                    nc.gpsimd.tensor_tensor(ring[:, n % RING, :, :], du[:, :, :],
                                            bc_all[:, n % 2, 0:1, :].to_broadcast([P, DB, T]), ALU.mult).then_inc(dbu, 1)
                    if n == 1 and kind != "first":
                        gate(CH - 1, 1 - q)
                    if n == 13 and kind != "last":
                        low_part(CH + 1)

            chunks(pool, body)
            gate(NCHUNK - 1, 1)

        @block.scalar
        def _(act):
            act.wait_ge(const_in, 16 * (len(consts) + 1))
            nc.scalar.activation(a_exp[:, :, :], a_exp[:, :, :], ACT.Exp).then_inc(a_act, 1)
            for b in range(BATCH):
                gn_scale(nc, "scalar", act, b, None, s, tiles[b])

            def front(at, n, CH, q):
                for name in FRONT.get(n, []):
                    k = int(name[-1]) if name != "XD" else 0
                    if name[0] == "U":
                        if k == 0:
                            act.wait_ge(halo, CH + 1)
                        act.wait_ge(wk_mm, at.mm(name))
                        nc.scalar.activation(u_raw[:, k, DC - 1:], at.bank(name), ACT.Copy).then_inc(wk_act, 1)
                    if name[0] == "Z":
                        act.wait_ge(wk_mm, at.mm(name))
                        at_least(act, y_pool, CH - 1)
                        nc.scalar.activation(z_act[:, q, k, :], at.bank(name), ACT.Copy).then_inc(wk_act, 1)
                    if name == "XD":
                        act.wait_ge(wk_mm, at.mm(name))
                        nc.scalar.activation(dt_low[4 * NS:5 * NS, :], at.bank(name)[4 * NS:5 * NS, :], ACT.Copy).then_inc(dt_act, 1)
                        nc.scalar.activation(bc[:, q, :], at.bank(name)[0:4 * NS, :], ACT.Copy).then_inc(wk_act, 1)
                    if name[0] == "D":
                        act.wait_ge(wk_mm, at.mm(name))
                        nc.scalar.activation(relu_v[:, k, :], at.bank(name), ACT.Relu, bias=s_bdt[:, k:k + 1]).then_inc(v_act, 1)
                        nc.scalar.activation(e_abs[:, k, :], at.bank(name), ACT.Abs, bias=s_bdt[:, k:k + 1]).then_inc(wk_act, 1)
                if n == 9:
                    act.wait_ge(conv, (CH + 1) * (DB * DC))
                    nc.scalar.activation(u_act[:, q, :, :], u_conv[:, :, :], ACT.Silu).then_inc(act_u, 1)
                    act.wait_ge(wk_act, at.act("Z3"))
                    nc.scalar.activation(z_act[:, q, :, :], z_act[:, q, :, :], ACT.Silu).then_inc(act_z, 1)
                if n == 12:
                    act.wait_ge(wk_act, at.act("DT3"))
                    nc.scalar.activation(e_abs[:, :, :], e_abs[:, :, :], ACT.Exp, scale=-1.0).then_inc(e_act, 1)
                if n == 13:
                    act.wait_ge(e_act, CH + 1)
                    nc.scalar.activation(log_e[:, :, :], e_abs[:, :, :], ACT.Ln, bias=1.0).then_inc(log_act, 1)

            def copy_row(at, n, k, CH):
                name = f"{'BC'[k]}{n % NS}"
                act.wait_ge(wk_mm, at.mm(name))
                at_least(act, (dbu, hc_done)[k], CH * NS + n - 1)
                nc.scalar.activation(bc_all[:, n % 2, k, :], at.bank(name), ACT.Copy).then_inc(wk_act, 1)

            pro = BankCount("pro", 0)
            for n in range(NS):
                front(pro, n, 0, 0)
            for k in range(2):
                copy_row(pro, 0, k, 0)

            def body(kind, b, c, CH, q):
                at = BankCount(kind, CH)
                act.wait_ge(delta_dve, CH + 1)
                act.wait_ge(a_dve, 1)
                for n in range(NS):
                    at_least(act, scan, CH * (NS * DB) + (n - 1) * DB)
                    for k in range(DB):
                        nc.scalar.activation(d_a[:, n % 2, k, :], delta[:, k, :], ACT.Exp, scale=a_neg[:, k, n:n + 1]).then_inc(da_act, 1)
                    if n + 1 < NS or kind != "last":
                        for k in range(2):
                            copy_row(at, n + 1, k, CH)
                    if kind != "last":
                        front(at, n, CH + 1, 1 - q)
                    if kind != "first":
                        post(at, n)

            def post(at, n):
                if n == 2:
                    for k in range(KT):
                        act.wait_ge(wk_mm, at.mm(f"OUT{k}"))
                        nc.scalar.activation(o_in[:, k, :], at.bank(f"OUT{k}"), ACT.Copy).then_inc(wk_act, 1)

            chunks(act, body)
            post(BankCount("epi", NCHUNK), 2)

        @block.vector
        def _(dve):
            dve.wait_ge(a_act, 1)
            nc.vector.tensor_scalar(a_neg[:, :, :], a_exp[:, :, :], -1.0, None, ALU.mult).then_inc(a_dve, 1)
            for b in range(BATCH):
                gn_stats(nc, dve, b, xn_all, all_in, s, tiles[b])
            for b in range(BATCH):
                gn_scale(nc, "vector", dve, b, None, s, tiles[b])
            nc.vector.memset(state[:, :, :], 0.0).then_inc(state0, 1)
            nc.vector.memset(u_raw[:, :, 0:DC - 1], 0.0).then_inc(halo, 1)

            def front(at, n, CH, q, b):
                if n == 0:
                    dve.wait_ge(xc_in, 16 * CH + 16)
                    for k in range(KT):
                        nc.vector.tensor_scalar(x_in_t[:, k, :], x_in_t[:, k, :], tiles[b]["mg"][:, k, 0:1], tiles[b]["rs"][:, k:k + 1],
                                                ALU.subtract, ALU.mult).then_inc(x_norm, 1)
                if n == 1:
                    for k in range(KT):
                        dve.wait_ge(wk_mm, at.mm(f"SEQ{k}"))
                        nc.vector.tensor_scalar(seq[:, k, :], at.bank(f"SEQ{k}"), s_bto[:, k:k + 1], None, ALU.add).then_inc(wk_dve, 1)
                if 5 <= n < 5 + DB:
                    k = n - 5
                    dve.wait_ge(wk_act, at.act(f"U{k}"))
                    for tap in range(DC):
                        src = u_raw[:, k, tap:tap + T]
                        if tap == 0:
                            nc.vector.tensor_scalar(u_conv[:, k, :], src, s_cw[:, k, 0:1], s_cb[:, k:k + 1],
                                                    ALU.mult, ALU.add).then_inc(conv, 1)
                        else:
                            dve.wait_ge(conv, CH * (DB * DC) + k * DC + tap)
                            nc.vector.scalar_tensor_tensor(out=u_conv[:, k, :], in0=src, scalar=s_cw[:, k, tap:tap + 1],
                                                           in1=u_conv[:, k, :], op0=ALU.mult, op1=ALU.add).then_inc(conv, 1)
                    if k == DB - 1:
                        if isinstance(CH, int) and (CH + 1) % NC == 0:
                            nc.vector.memset(u_raw[:, :, 0:DC - 1], 0.0).then_inc(halo, 1)
                        else:
                            nc.vector.tensor_copy(u_raw[:, :, 0:DC - 1], u_raw[:, :, T:T + DC - 1]).then_inc(halo, 1)
                if n == 10:
                    dve.wait_ge(wk_act, at.act("XD"))
                    nc.vector.tensor_tensor(bc[2 * NS:4 * NS, q, :], at.bank("XD")[2 * NS:4 * NS, :], bc[2 * NS:4 * NS, q, :],
                                            ALU.subtract).then_inc(wk_dve, 1)
                if n == 12:
                    dve.wait_ge(e_act, CH + 1)
                    dve.wait_ge(act_u, CH + 1)
                    nc.vector.tensor_scalar(low_e[:, :, :], e_abs[:, :, :], 1.0, -1.0, ALU.add, ALU.add).then_inc(one_dve, 1)
                if n == 15:
                    dve.wait_ge(log_act, CH + 1)
                    dve.wait_ge(low_pool, CH + 1)
                    nc.vector.tensor_tensor(log_e[:, :, :], log_e[:, :, :], low_e[:, :, :], ALU.subtract).then_inc(sum_dve, 1)

            def seam(CH, q):
                at_least(dve, da_act, CH * (NS * DB))
                at_least(dve, dbu, CH * NS)
                dve.wait_ge(sum_dve, CH + 1)
                dve.wait_ge(v_act, (CH + 1) * DB)
                nc.vector.tensor_tensor(delta[:, :, :], relu_v[:, :, :], log_e[:, :, :], ALU.add).then_inc(delta_dve, 1)
                dve.wait_ge(delta_dve, CH + 1)
                nc.vector.tensor_tensor(du[:, :, :], delta[:, :, :], u_act[:, q, :, :], ALU.mult).then_inc(du_dve, 1)

            def skip(CH, q):
                dve.wait_ge(y_mm, (CH + 1) * NS)
                for k in range(DB):
                    nc.vector.scalar_tensor_tensor(out=y[:, k, :], in0=u_act[:, q, k, :], scalar=s_d[:, k:k + 1],
                                                   in1=yp[:, k, :], op0=ALU.mult, op1=ALU.add).then_inc(yd_dve, 1)

            def residual(at, CH):
                dve.wait_ge(res_in, 16 * CH + 16)
                for k in range(KT):
                    dve.wait_ge(wk_mm, at.mm(f"FROM{k}"))
                    nc.vector.scalar_tensor_tensor(out=x_res[:, k, :], in0=at.bank(f"FROM{k}"), scalar=s_bfrom[:, k:k + 1],
                                                   in1=x_res[:, k, :], op0=ALU.add, op1=ALU.add).then_inc(wk_dve, 1)

            for n in range(NS):
                front(BankCount("pro", 0), n, 0, 0, 0)
            seam(0, 0)

            def body(kind, b, c, CH, q):
                at = BankCount(kind, CH)
                if isinstance(CH, int) and CH % NC == 0 and CH > 0:
                    dve.wait_ge(st_dve, CH * NS)
                    nc.vector.memset(state[:, :, :], 0.0).then_inc(state0, 1)
                for n in range(NS):
                    r = n % RING
                    dve.wait_ge(dbu, CH * NS + n + 1)
                    if n == 0:
                        at_least(dve, st_dve, CH * NS)
                        dve.wait_ge(state0, b + 1)
                    for k in range(DB):
                        dve.wait_ge(da_act, CH * (NS * DB) + n * DB + k + 1)
                        nc.vector.tensor_tensor_scan(ring[:, r, k, :], d_a[:, n % 2, k, :], ring[:, r, k, :],
                                                     state[:, k, n:n + 1], ALU.mult, ALU.add).then_inc(scan, 1)
                    dve.wait_ge(scan, CH * (NS * DB) + (n + 1) * DB)
                    nc.vector.tensor_copy(state[:, :, n], ring[:, r, :, T - 1]).then_inc(st_dve, 1)
                    if n == 0 and kind != "first":
                        skip(CH - 1, 1 - q)
                    if kind != "last":
                        front(at, n, CH + 1, 1 - q, (b + 1 if c == NC - 1 else b) if isinstance(c, int) else b)
                    dve.wait_ge(st_dve, CH * NS + n + 1)
                    if n == 0:
                        c_ready = BankCount("pro", 0).act("C0") if kind == "first" else at.before(scalar_holds)
                    else:
                        c_ready = at.act(f"C{n}")
                    dve.wait_ge(wk_act, c_ready)
                    nc.vector.tensor_tensor(ring[:, r, :, :], ring[:, r, :, :],
                                            bc_all[:, n % 2, 1:2, :].to_broadcast([P, DB, T]), ALU.mult).then_inc(hc_done, 1)
                    if n == 3 and kind != "first":
                        residual(at, CH - 1)
                if kind != "last":
                    seam(CH + 1, 1 - q)

            chunks(dve, body)
            skip(NCHUNK - 1, 1)
            residual(BankCount("epi", NCHUNK), NCHUNK - 1)

        @block.tensor
        def _(pe):
            pe.wait_ge(const_in, 16 * (len(consts) + 1))
            pe.wait_ge(hot_in, 16)
            for b in range(BATCH):
                gn_scale(nc, "tensor", pe, b, None, s, tiles[b])
            pe.wait_ge(s["gn_dve"], GN_ALL)

            def bank_free(at, name):
                units = ORDER[at.kind]
                i = units.index(name)
                if i < 4:
                    at_least(pe, wk_act, at.before(scalar_holds))
                    at_least(pe, wk_dve, at.before(vector_holds))
                elif vector_holds(units[i - 4]):
                    pe.wait_ge(wk_dve, at.dve(units[i - 4]))
                else:
                    pe.wait_ge(wk_act, at.act(units[i - 4]))

            def project(at, name, w, m, src, k_tiles):
                bank_free(at, name)
                for k in range(k_tiles):
                    mm = nc.tensor.matmul(at.bank(name), w[:, k, m * P:(m + 1) * P], src(k), start=(k == 0), stop=(k == k_tiles - 1))
                mm.then_inc(wk_mm, 1)

            def front(at, n, CH, q):
                for name in FRONT.get(n, []):
                    m = int(name[-1]) if name != "XD" else 0
                    if name == "SEQ0":
                        pe.wait_ge(x_norm, KT * CH + KT)
                    if name == "U0":
                        pe.wait_ge(wk_dve, at.dve("SEQ1"))
                    if name[0] == "S":
                        project(at, name, s_to, m, lambda k: x_in_t[:, k, :], KT)
                    if name[0] == "U":
                        project(at, name, s_in, m, lambda k: seq[:, k, :], KT)
                    if name[0] == "Z":
                        project(at, name, s_in, DB + m, lambda k: seq[:, k, :], KT)
                    if name == "XD":
                        pe.wait_ge(act_u, CH + 1)
                        bank_free(at, name)
                        for k in range(DB):
                            mm = nc.tensor.matmul(at.bank(name)[0:5 * NS, :], s_x[:, k, :], u_act[:, q, k, :], start=(k == 0), stop=(k == DB - 1))
                        mm.then_inc(wk_mm, 1)
                    if name[0] == "D":
                        if m == 0:
                            pe.wait_ge(dt_act, CH + 1)
                        bank_free(at, name)
                        nc.tensor.matmul(at.bank(name), s_dt[4 * NS:5 * NS, m * P:(m + 1) * P], dt_low[4 * NS:5 * NS, :],
                                         start=True, stop=True).then_inc(wk_mm, 1)

            def post(at, n, CH):
                if n == 2:
                    pe.wait_ge(y_pool, CH + 1)
                    for m in range(KT):
                        project(at, f"OUT{m}", s_out, m, lambda k: y[:, k, :], DB)
                if n == 3:
                    pe.wait_ge(wk_act, at.act("OUT1"))
                    for m in range(KT):
                        project(at, f"FROM{m}", s_from, m, lambda k: o_in[:, k, :], KT)

            def copy_rows(at, n, q):
                for k in range(2):
                    name = f"{'BC'[k]}{n % NS}"
                    bank_free(at, name)
                    nc.tensor.matmul(at.bank(name), s_pick[:, k * NS + n % NS, :], bc[:, q, :], start=True, stop=True).then_inc(wk_mm, 1)

            pro = BankCount("pro", 0)
            for n in range(NS):
                front(pro, n, 0, 0)
            pe.wait_ge(wk_dve, pro.dve("XD"))
            copy_rows(pro, 0, 0)

            def body(kind, b, c, CH, q):
                at = BankCount(kind, CH)

                def add_up(n):
                    pe.wait_ge(hc_done, CH * NS + n + 1)
                    if n == 0:
                        at_least(pe, yd_dve, CH * DB)
                    for k in range(DB):
                        mm = nc.tensor.matmul(yp[:, k, :], ident[:, :], ring[:, n % RING, k, :], start=(n == 0), stop=(n == NS - 1))
                    mm.then_inc(y_mm, 1)

                for n in range(NS):
                    if n + 1 < NS:
                        copy_rows(at, n + 1, q)
                    elif kind != "last":
                        pe.wait_ge(wk_dve, at.dve("XD"))
                        copy_rows(at, n + 1, 1 - q)
                    if kind != "last":
                        front(at, n, CH + 1, 1 - q)
                    if kind != "first":
                        post(at, n, CH - 1)
                    if n >= 1:
                        add_up(n - 1)
                add_up(NS - 1)

            chunks(pe, body)
            for n in (2, 3):
                post(BankCount("epi", NCHUNK), n, NCHUNK - 1)


ATT_IN = ["w_qk", "w_v", "height_rel", "width_rel", "key_hot", "pos_hot", "identity", "group_mean"]
MAM_IN = ["w_to", "b_to", "w_in", "conv_w", "conv_b", "w_x", "w_dt", "b_dt", "a_log", "d_skip", "w_out", "w_from", "b_from",
          "identity", "group_mean", "pick"]


def lay_out(inputs):
    import numpy as np

    a = {k: np.asarray(v) for k, v in inputs.items()}
    w = a["L0_conv_qkv_w"]
    key = np.arange(L)
    key_hot = (key[None, :] % WW == np.arange(WW)[:, None]).astype(np.float32)
    row_hot = (key[None, :L // 2] // WW == np.arange(HH // 2)[:, None]).astype(np.float32)
    channel = np.arange(P)

    def rows(v):
        return np.ascontiguousarray(np.swapaxes(v.reshape(v.shape[0] // P, P, *v.shape[1:]), 0, 1))

    w_x = a["L1_conv_x_proj_w"].T
    w_dt_cols, w_bc_cols = w_x[:, :DR], w_x[:, DR:]
    pick = np.zeros((2, 2 * NS, 2 * NS, P), np.float32)
    pick[:, np.arange(2 * NS), np.arange(2 * NS), :] = 1
    return {
        "x": a["x"].reshape(BATCH, C, L),
        "w_qk": np.ascontiguousarray(w[:2 * C].reshape(2, HEADS, D, C).transpose(3, 1, 0, 2)),
        "w_v": np.ascontiguousarray(w[2 * C:].T.reshape(KT, P, C).transpose(1, 0, 2)),
        "height_rel": np.ascontiguousarray(a["L0_conv_height_rel"].T),
        "width_rel": np.ascontiguousarray(a["L0_conv_width_rel"].T),
        "key_hot": key_hot,
        "pos_hot": np.concatenate([key_hot[:, :L // 2], row_hot, row_hot]),
        "identity": np.eye(P, dtype=np.float32),
        "group_mean": (channel[:, None] // 8 == channel[None, :] // 8).astype(np.float32) / 8,
        "w_to": rows(a["L1_conv_to_seq_w"].T),
        "b_to": rows(a["L1_conv_to_seq_b"]),
        "w_in": rows(a["L1_conv_in_proj_w"].T),
        "conv_w": rows(a["L1_conv_conv_w"]),
        "conv_b": rows(a["L1_conv_conv_b"]),
        "w_x": rows(np.concatenate([w_bc_cols, w_bc_cols, w_dt_cols], axis=1)),
        "w_dt": np.ascontiguousarray(a["L1_conv_dt_proj_w"].T),
        "b_dt": rows(a["L1_conv_dt_proj_b"]),
        "a_log": rows(a["L1_conv_A_log"]),
        "d_skip": rows(a["L1_conv_D"]),
        "w_out": rows(a["L1_conv_out_proj_w"].T),
        "w_from": rows(a["L1_conv_from_seq_w"].T),
        "b_from": rows(a["L1_conv_from_seq_b"]),
        "pick": pick.reshape(4 * NS, 2 * NS, P),
    }


def kernel(**inputs):
    import numpy as np
    from concourse import bacc
    from concourse.bass_utils import run_bass_kernel_spmd

    arrays = lay_out(inputs)
    nc = bacc.Bacc("TRN2", target_bir_lowering=False, num_devices=1)
    dram = {n: nc.dram_tensor(n, v.shape, mybir.dt.from_np(v.dtype), kind="ExternalInput").ap() for n, v in arrays.items()}
    x1 = nc.dram_tensor("x1", [BATCH, C, L], F32).ap()
    out = nc.dram_tensor("out", [BATCH, C, L], F32, kind="ExternalOutput").ap()
    attention_layer(nc, dram["x"], x1, *[dram[n] for n in ATT_IN])
    mamba_layer(nc, x1, out, *[dram[n] for n in MAM_IN])
    r = run_bass_kernel_spmd(nc, [arrays], core_ids=[0])
    return r.results[0]["out"].reshape(BATCH, C, HH, WW)
```

```python
from contextlib import ExitStack

import concourse.bass as bass
from concourse import mybir

F32 = mybir.dt.float32
F32R = mybir.dt.float32r
ALU = mybir.AluOpType
ACT = mybir.ActivationFunctionType
AX = mybir.AxisListType

BATCH, C, HH, WW = 2, 256, 64, 64
L = HH * WW
P = 128
KT = C // P
EPS = 1e-5

HEADS, D = 4, 64
SCALE = float(D) ** -0.5
QB = 512
NB = L // QB
QT = QB // P
NKT = L // P
GK = 2
NG = NKT // GK
NCH = L // 512
REL = 2 * WW - 1
YQ = QB // WW
PREP_UNITS = 28
PREP_ACT, PREP_DVE, BLK_ACT = 36, 20, 3

DI, NS, DC, DR = 512, 16, 4, 16
DB = DI // P
T = 512
NC = L // T
GN_STATS, GN_SCALE = KT * (L // 512) + KT, 5
GN_DVE = GN_STATS + GN_SCALE + KT


def stand_apart(e, passed):
    e.sem_inc(passed, 1)


def gn_stats(nc, e, base, xn, s, t):
    for k in range(KT):
        for j in range(L // 512):
            nc.vector.bn_stats(t["st"][:, k, j, :], xn[:, k, j * 512:(j + 1) * 512]).then_inc(s["gn_dve"], 1)
    e.wait_ge(s["gn_dve"], base + GN_STATS - KT)
    stand_apart(e, t["passed"])
    for k in range(KT):
        nc.vector.bn_aggr(t["mv"][:, k, :], t["st"][:, k, :, :].rearrange("p a b -> p (a b)")).then_inc(s["gn_dve"], 1)


def gn_scale(nc, role, e, base, n, s, t):
    done = base + GN_STATS
    if role == "vector":
        e.wait_ge(s["gn_pe"], 2 * n + 1)
        nc.vector.tensor_copy(t["mg"][:, :, :], t["gps"][:, 0:2 * KT].rearrange("p (k m) -> p k m", k=KT)).then_inc(s["gn_dve"], 1)
        e.wait_ge(s["gn_dve"], done + 1)
        nc.vector.tensor_tensor(t["df"][:, :], t["mv"][:, :, 0], t["mg"][:, :, 0], ALU.subtract).then_inc(s["gn_dve"], 1)
        e.wait_ge(s["gn_dve"], done + 2)
        nc.vector.tensor_tensor(t["sq"][:, :], t["df"][:, :], t["df"][:, :], ALU.mult).then_inc(s["gn_dve"], 1)
        e.wait_ge(s["gn_pe"], 2 * n + 2)
        nc.vector.scalar_tensor_tensor(out=t["va"][:, :], in0=t["gps"][:, 0:KT], scalar=EPS, in1=t["mg"][:, :, 1],
                                       op0=ALU.add, op1=ALU.add).then_inc(s["gn_dve"], 1)
        e.wait_ge(s["gn_act"], n + 1)
        nc.vector.reciprocal(t["rs"][:, :], t["sd"][:, :]).then_inc(s["gn_dve"], 1)
        e.wait_ge(s["gn_dve"], done + GN_SCALE)
    elif role == "tensor":
        e.wait_ge(s["gn_dve"], done)
        nc.tensor.matmul(t["gps"][:, 0:2 * KT], t["gavg"][:, :], t["mv"][:, :, :].rearrange("p k m -> p (k m)"),
                         start=True, stop=True).then_inc(s["gn_pe"], 1)
        e.wait_ge(s["gn_dve"], done + 3)
        nc.tensor.matmul(t["gps"][:, 0:KT], t["gavg"][:, :], t["sq"][:, :], start=True, stop=True).then_inc(s["gn_pe"], 1)
    elif role == "scalar":
        e.wait_ge(s["gn_dve"], done + 4)
        nc.scalar.activation(t["sd"][:, :], t["va"][:, :], ACT.Sqrt).then_inc(s["gn_act"], 1)


def gn_tiles(sb, layer):
    return {"st": sb(layer + "_gn_stats", [P, KT, L // 512, 6]), "mv": sb(layer + "_gn_meanvar", [P, KT, 2]),
            "mg": sb(layer + "_gn_group", [P, KT, 2]), "df": sb(layer + "_gn_diff", [P, KT]), "sq": sb(layer + "_gn_square", [P, KT]),
            "va": sb(layer + "_gn_var", [P, KT]), "sd": sb(layer + "_gn_sd", [P, KT]), "rs": sb(layer + "_gn_rstd", [P, KT])}


def attention_layer(nc, x, x1, w_qk, w_v, height_rel, width_rel, key_hot, pos_hot, identity, group_mean):
    with ExitStack() as ctx:
        def sb(name, shape, dt=F32):
            return ctx.enter_context(nc.sbuf_tensor(name, shape, dt))

        def sem(name):
            return ctx.enter_context(nc.semaphore(name))

        xn = sb("a_xn", [P, KT, L])
        k_pos = sb("a_k_pos", [P, L], F32R)
        k_hl = sb("a_k_hl", [P, L], F32R)
        pos = sb("a_pos", [P, L // 2], F32R)
        v_hl = sb("a_v_hl", [P, NKT, P], F32R)
        q_all = sb("a_q", [D, L])
        w_all = sb("a_w", [P, L], F32R)
        m_hi = sb("a_m_hi", [P, 2, QB], F32R)
        m_lo = sb("a_m_lo", [P, 2, QB], F32R)
        m_pos = sb("a_m_pos", [P, 2, 2, QB], F32R)
        q_blk = sb("a_q_blk", [D, QB])
        probs = sb("a_probs", [P, 2, GK, QB])
        p_hi = sb("a_p_hi", [P, 4, GK, QB], F32R)
        p_lo = sb("a_p_lo", [P, 4, GK, QB], F32R)
        p_sum = sb("a_p_sum", [P, 2, GK, QB])
        w_head = sb("a_w_head", [P, KT, 2, D])
        w_val = sb("a_w_val", [P, KT, D])
        hrel = sb("a_hrel", [D, REL + 1])
        wrel = sb("a_wrel", [D, REL + 1])
        ident = sb("a_ident", [P, P])
        gavg = sb("a_gavg", [P, P])
        col_max = sb("a_col_max", [P, QT, HH])
        row_sum = sb("a_row_sum", [P, QT, HH])
        q_max = sb("a_q_max", [P, QT])
        r_less = sb("a_r_less", [P, QT, 3 * D])
        rh = sb("a_rh", [P, QT, 66])
        ones = sb("a_ones", [P, D])
        weighed = sb("a_weighed", [D, QB])
        rec = sb("a_rec", [P, QT])
        x_res = sb("a_x_res", [D, 2, QB])
        t = gn_tiles(sb, "a")
        t["gavg"] = gavg

        sc = ctx.enter_context(nc.psum_tensor("a_scores", [P, 2, GK, QB], F32))
        mx = ctx.enter_context(nc.psum_tensor("a_mx", [P, 2, 512], F32))
        oa = ctx.enter_context(nc.psum_tensor("a_oa", [P, QB], F32))
        mi = ctx.enter_context(nc.psum_tensor("a_mi", [P, 512], F32))
        t["gps"] = mi
        rh_ps = mx[:, 0, 0:QT * 66].rearrange("p (t r) -> p t r", t=QT)

        s = {n: sem("a_" + n) for n in ("gn_dve", "gn_pe", "gn_act")}
        const_in, x_in, wh_in = (sem("a_" + n) for n in ("const_in", "x_in", "wh_in"))
        res_in, x1_out = ([sem(f"a_{n}{k}") for k in range(2)] for n in ("res_in", "x1_out"))
        ones_set, hot_in = sem("a_ones_set"), sem("a_hot_in")
        passed = t["passed"] = sem("a_passed")
        proj_mm, prep_act, prep_dve, prep_pool = (sem("a_" + n) for n in ("proj_mm", "prep_act", "prep_dve", "prep_pool"))
        first_act, blk_act, rh_dve = (sem("a_" + n) for n in ("first_act", "blk_act", "rh_dve"))
        blk_pool, mx_mm, mx_red, rh_mm, sum_dve, max_dve, rp_dve, tr_mm, hi_act, lo_dve = (
            sem("a_" + n) for n in ("blk_pool", "mx_mm", "mx_red", "rh_mm", "sum_dve", "max_dve", "rp_dve", "tr_mm",
                                    "hi_act", "lo_dve"))
        score_mm, exp_act, lo_p, sum_pool, pv_mm, half_dve, oa_read, total_mm, rec_dve, spread_mm, norm_dve, out_pool = (
            sem("a_" + n) for n in ("score_mm", "exp_act", "lo_p", "sum_pool", "pv_mm", "half_dve", "oa_read", "total_mm",
                                    "rec_dve", "spread_mm", "norm_dve", "out_pool"))
        EXP0, LO0, SUM0 = 4, 2, 2

        def exp_count(B, g, which):
            return EXP0 + 2 * (B * NG + g) + which

        MAX_COUNT = (0, 2, 2, 3, 2, 3, 3, 3, 3, 3, 3, 3, 2, 0, 0, 0)
        MAX_AT = [range(sum(MAX_COUNT[:g]), sum(MAX_COUNT[:g + 1])) for g in range(NG)]
        LAST_WEIGHED = ((NG - 3, NG - 2), (NG - 1,), ())
        HEIGHT_AT, HEIGHT_COPY_AT, LESS_AT, TURN_AT, R_HI_AT, R_LO_AT, TAKE_AT = 0, 1, 13, 14, 14, 15, 2
        N_CONST = 4

        def v_stage(pair):
            return probs[:, pair // GK, pair % GK, :]

        def v_tiles(u):
            return unit_bank(u).rearrange("p (t e d) -> p e t d", t=4, e=2)

        def v_part(u, lo):
            return v_hl[:, 8 * (u - 24):8 * (u - 23), lo * D:lo * D + D].rearrange("p (e t) d -> p e t d", e=2)

        def unit_bank(u):
            return sc[:, (u % 4) // 2, u % 2, :]

        def main_blocks(e, body):
            body(0, 0, 0, 2)
            body(0, 1, 1, 2)
            with e.Fori(1, NB // 2 - 1) as ii:
                body(ii, 0, 2, 2)
                body(ii, 1, 2, 2)
            body(NB // 2 - 1, 0, 2, 1)
            body(NB // 2 - 1, 1, 2, 0)

        block = ctx.enter_context(nc.Block())

        @block.sync
        def _(sp):
            for dst, src in ((hrel[:, 0:REL], height_rel), (wrel[:, 0:REL], width_rel),
                             (ident[:, :], identity), (gavg[:, :], group_mean)):
                sp.dma_start(dst, src).then_inc(const_in, 16)
            with sp.Fori(0, BATCH) as b:
                sp.wait_ge(proj_mm, b * (HEADS * PREP_UNITS))
                sp.dma_start(xn[:, :, :], x[bass.ds(b, 1), :, :].rearrange("o (k p) l -> (o p) k l", p=P)).then_inc(x_in, 16)
                with sp.Fori(0, HEADS) as h:
                    H = b * HEADS + h
                    sp.wait_ge(proj_mm, H * PREP_UNITS)
                    for k in range(KT):
                        for role in range(2):
                            sp.dma_start(w_head[:, k, 1 - role, :], w_qk[k * P:(k + 1) * P, bass.ds(h, 1), role, :]
                                         .rearrange("p o d -> p (o d)")).then_inc(wh_in, 16)
                    sp.dma_start(w_val[:, :, :], w_v[:, :, bass.ds(h * D, D)]).then_inc(wh_in, 16)
                    for i in range(NB):
                        sp.wait_ge(x1_out[i % 2], H * (8 * NB) + 16 * (i // 2))
                        sp.dma_start(x_res[:, i % 2, :], x[bass.ds(b, 1), bass.ds(h * D, D), i * QB:(i + 1) * QB]
                                     .rearrange("o c l -> (o c) l")).then_inc(res_in[i % 2], 16)
            for k in range(2):
                sp.wait_ge(x1_out[k], 8 * BATCH * HEADS * NB)

        @block.gpsimd
        def _(pool):
            pool.dma_start(pos[:, :], pos_hot).then_inc(hot_in, 16)
            pool.dma_start(k_pos[D:P, :], key_hot).then_inc(hot_in, 16)
            nc.gpsimd.memset(ones[:, :], 1.0).then_inc(ones_set, 1)
            nc.gpsimd.memset(r_less[:, :, 0:D], 0.0).then_inc(ones_set, 1)
            pool.sem_inc(sum_pool, SUM0)

            def q_low(H, i, sl, sums_done):
                B = H * NB + i
                pool.wait_ge(sum_pool, SUM0 + sums_done)
                pool.wait_ge(first_act, 3 * B + 2)
                stand_apart(pool, passed)
                nc.gpsimd.tensor_tensor(m_lo[0:D, sl, :], q_all[:, bass.ds(i * QB, QB)], m_hi[0:D, sl, :], ALU.subtract).then_inc(blk_pool, 1)
                pool.wait_ge(blk_pool, B + 1)

            with pool.Fori(0, BATCH) as b:
                with pool.Fori(0, HEADS) as h:
                    H = b * HEADS + h
                    for c in range(NCH):
                        pool.wait_ge(prep_act, H * PREP_ACT + 2 * c + 1)
                        stand_apart(pool, passed)
                        nc.gpsimd.tensor_copy(k_pos[0:D, c * 512:(c + 1) * 512], k_hl[0:D, c * 512:(c + 1) * 512]).then_inc(prep_pool, 1)
                    q_low(H, 0, 0, H * NB * NG)

                    def finish(done, i, sl):
                        pool.wait_ge(norm_dve, done)
                        pool.wait_ge(res_in[sl], H * (8 * NB) + 8 * (i - sl) + 16)
                        stand_apart(pool, passed)
                        nc.gpsimd.tensor_tensor(x_res[:, sl, :], weighed[:, :], x_res[:, sl, :], ALU.add).then_inc(out_pool, 1)
                        pool.wait_ge(out_pool, done)
                        pool.dma_start(x1[bass.ds(b, 1), bass.ds(h * D, D), bass.ds(i * QB, QB)].rearrange("o c l -> (o c) l"),
                                       x_res[:, sl, :]).then_inc(x1_out[sl], 16)

                    def body(ii, sl, before, after):
                        i = 2 * ii + sl
                        B = H * NB + i
                        for g in range(1, NG):
                            pool.wait_ge(exp_act, exp_count(B, g, 1))
                            if g == 1:
                                if before:
                                    pool.wait_ge(total_mm, B - 1)
                                nc.gpsimd.tensor_tensor(p_sum[:, sl, :, :], probs[:, 0, :, :], probs[:, 1, :, :],
                                                        ALU.add).then_inc(sum_pool, 2)
                                if after:
                                    q_low(H, i + 1, 1 - sl, B * NG + 2)
                            else:
                                pool.wait_ge(sum_pool, SUM0 + B * NG + g)
                                nc.gpsimd.tensor_tensor(p_sum[:, sl, :, :], p_sum[:, sl, :, :], probs[:, g % 2, :, :],
                                                        ALU.add).then_inc(sum_pool, 1)
                            if g == 7 and before:
                                finish(B, i - 1, 1 - sl)
                        if not after:
                            finish(B + 1, i, sl)

                    main_blocks(pool, body)

        @block.scalar
        def _(act):
            act.sem_inc(exp_act, EXP0)

            def first_operands(H, i, sl):
                blk = bass.ds(i * QB, QB)
                act.wait_ge(rh_mm, H * NB + i)
                nc.scalar.activation(q_blk[:, :], q_all[:, blk], ACT.Copy).then_inc(first_act, 1)
                nc.scalar.activation(m_hi[0:D, sl, :], q_all[:, blk], ACT.Copy).then_inc(first_act, 1)
                nc.scalar.activation(m_hi[D:P, sl, :], w_all[D:P, blk], ACT.Copy).then_inc(first_act, 1)

            def other_operand(i, sl, n):
                blk = bass.ds(i * QB, QB)
                dst, src = ((m_lo[D:P, sl, :], q_all[:, blk]), (m_pos[0:D, sl, 0, :], w_all[0:D, blk]),
                            (m_pos[0:D, sl, 1, :], w_all[0:D, blk]))[n]
                nc.scalar.activation(dst, src, ACT.Copy).then_inc(blk_act, 1)

            with act.Fori(0, BATCH) as b:
                gn_scale(nc, "scalar", act, b * GN_DVE, b, s, t)
                with act.Fori(0, HEADS) as h:
                    H = b * HEADS + h
                    for u in range(NCH):
                        act.wait_ge(proj_mm, H * PREP_UNITS + u + 1)
                        cols = slice(u * 512, (u + 1) * 512)
                        nc.scalar.activation(k_hl[0:D, cols], unit_bank(u)[0:D, :], ACT.Copy, scale=SCALE).then_inc(prep_act, 1)
                        nc.scalar.activation(q_all[:, cols], unit_bank(u)[D:P, :], ACT.Copy).then_inc(prep_act, 1)
                    for u in range(8, 16):
                        act.wait_ge(proj_mm, H * PREP_UNITS + u + 1)
                        nc.scalar.activation(w_all[D:P, :].rearrange("p (y x) -> p x y", x=WW)[:, 8 * (u - 8):8 * (u - 7), :],
                                             unit_bank(u)[D:P, :].rearrange("p (x y) -> p x y", x=8), ACT.Copy).then_inc(prep_act, 1)
                    act.wait_ge(prep_act, H * PREP_ACT + 24)
                    first_operands(H, 0, 0)
                    act.wait_ge(prep_dve, H * PREP_DVE + 16)
                    for n in range(3):
                        other_operand(0, 0, n)

                    act.wait_ge(lo_p, LO0 + H * NB * NG)
                    act.wait_ge(sum_pool, SUM0 + H * NB * NG)
                    for u in range(16, 24):
                        act.wait_ge(proj_mm, H * PREP_UNITS + u + 1)
                        half = slice(u % 2 * D, u % 2 * D + D)
                        nc.scalar.activation(v_stage((u - 16) // 2)[half, :], unit_bank(u)[0:D, :], ACT.Copy).then_inc(prep_act, 1)

                    def value_hi(u):
                        act.wait_ge(proj_mm, H * PREP_UNITS + u + 1)
                        nc.scalar.activation(v_part(u, 0), v_tiles(u), ACT.Copy).then_inc(prep_act, 1)


                    def r_hi(B, sl):
                        act.wait_ge(tr_mm, B + 1)
                        nc.scalar.activation(m_pos[D:P, sl, :, :], mx[D:P, :, :], ACT.Copy).then_inc(hi_act, 1)

                    value_hi(24)
                    value_hi(25)
                    first_operands(H, 1, 1)
                    r_hi(H * NB, 0)
                    value_hi(26)
                    value_hi(27)

                    def body(ii, sl, before, after):
                        i = 2 * ii + sl
                        B = H * NB + i
                        for g in range(NG):
                            act.wait_ge(score_mm, B * NG + g + 1)
                            act.wait_ge(lo_p, LO0 + B * NG + g - 1)
                            act.wait_ge(sum_pool, SUM0 + B * NG + g - 1)
                            nc.scalar.activation(probs[:, g % 2, :, :], sc[:, g % 2, :, :], ACT.Exp).then_inc(exp_act, 1)
                            nc.scalar.activation(p_hi[:, g % 4, :, :], sc[:, g % 2, :, :], ACT.Exp).then_inc(exp_act, 1)
                            if after and 1 <= g <= 3:
                                other_operand(i + 1, 1 - sl, g - 1)
                            if after and g == R_HI_AT:
                                r_hi(B + 1, 1 - sl)
                            if after == 2 and g == NG - 1:
                                first_operands(H, i + 2, sl)

                    main_blocks(act, body)

        @block.vector
        def _(dve):
            dve.sem_inc(lo_p, LO0)
            with dve.Fori(0, BATCH) as b:
                dve.wait_ge(x_in, 16 * b + 16)
                gn_stats(nc, dve, b * GN_DVE, xn, s, t)
                gn_scale(nc, "vector", dve, b * GN_DVE, b, s, t)
                for k in range(KT):
                    nc.vector.tensor_scalar(xn[:, k, :], xn[:, k, :], t["mg"][:, k, 0:1], t["rs"][:, k:k + 1],
                                            ALU.subtract, ALU.mult).then_inc(s["gn_dve"], 1)
                with dve.Fori(0, HEADS) as h:
                    H = b * HEADS + h
                    for u in range(NCH):
                        dve.wait_ge(prep_act, H * PREP_ACT + 2 * u + 1)
                        cols = slice(u * 512, (u + 1) * 512)
                        nc.vector.scalar_tensor_tensor(out=k_hl[D:P, cols], in0=unit_bank(u)[0:D, :], scalar=SCALE,
                                                       in1=k_hl[0:D, cols], op0=ALU.mult, op1=ALU.subtract).then_inc(prep_dve, 1)
                    for u in range(8, 16):
                        dve.wait_ge(prep_act, H * PREP_ACT + 8 + u + 1)
                        hi, lo = (w_all[r, :].rearrange("p (y x) -> p x y", x=WW)[:, 8 * (u - 8):8 * (u - 7), :]
                                  for r in (slice(D, P), slice(0, D)))
                        nc.vector.tensor_tensor(lo, unit_bank(u)[D:P, :].rearrange("p (x y) -> p x y", x=8), hi,
                                                ALU.subtract).then_inc(prep_dve, 1)

                    def height_copy(B):
                        dve.wait_ge(rh_mm, B + 1)
                        nc.vector.tensor_copy(rh[:, :, 0:HH + 1], rh_ps[:, :, 0:HH + 1]).then_inc(rh_dve, 1)

                    def column_max(B, ks):
                        for k in ks:
                            qt, c = divmod(k, NCH)
                            dve.wait_ge(mx_mm, B * (QT * NCH) + k + 1)
                            nc.vector.tensor_reduce(col_max[:, qt, c * 8:(c + 1) * 8],
                                                    mx[:, k % 2, :].rearrange("p (y x) -> p y x", x=WW), AX.X, ALU.max).then_inc(mx_red, 1)

                    def less_max(B):
                        dve.wait_ge(rh_dve, B + 1)
                        dve.wait_ge(mx_red, B * (QT * NCH) + QT * NCH)
                        for half in range(2):
                            r = slice(half * D, half * D + D)
                            nc.vector.tensor_tensor(row_sum[r, :, :], rh[r, :, 1 - half:1 - half + HH], col_max[r, :, :], ALU.add).then_inc(sum_dve, 1)
                        dve.wait_ge(sum_dve, 2 * B + 2)
                        nc.vector.tensor_reduce(q_max[:, :], row_sum[:, :, :], AX.X, ALU.max).then_inc(max_dve, 1)
                        dve.wait_ge(max_dve, B + 1)
                        for half in range(2):
                            r = slice(half * D, half * D + D)
                            for kh in range(2):
                                c0 = 1 - half + kh * 32
                                nc.vector.tensor_tensor(r_less[r, :, D + kh * D:2 * D + kh * D].rearrange("p t (a y) -> p t a y", a=2),
                                                        rh[r, :, c0:c0 + 32].unsqueeze(2).to_broadcast([D, QT, 2, 32]),
                                                        q_max[r, :].unsqueeze(2).unsqueeze(3).to_broadcast([D, QT, 2, 32]),
                                                        ALU.subtract).then_inc(rp_dve, 1)

                    def r_lo(B, sl):
                        dve.wait_ge(hi_act, B + 1)
                        nc.vector.tensor_tensor(m_pos[96:P, sl, :, :], mx[96:P, :, :], m_pos[96:P, sl, :, :], ALU.subtract).then_inc(lo_dve, 1)

                    def low_probs(B, g):
                        dve.wait_ge(exp_act, exp_count(B, g, 2))
                        nc.vector.tensor_tensor(p_lo[:, g % 4, :, :], probs[:, g % 2, :, :], p_hi[:, g % 4, :, :],
                                                ALU.subtract).then_inc(lo_p, 1)

                    def take_weighed(done):
                        dve.wait_ge(pv_mm, done * NG)
                        dve.wait_ge(out_pool, done - 1)
                        nc.vector.tensor_copy(weighed[:, :], oa[D:P, :]).then_inc(half_dve, 1)
                        dve.wait_ge(half_dve, done)
                        nc.vector.tensor_tensor(weighed[:, :], oa[0:D, :], weighed[:, :], ALU.add).then_inc(oa_read, 1)

                    def invert_totals(done):
                        dve.wait_ge(total_mm, done)
                        nc.vector.reciprocal(rec[:, :], mi[:, 0:QT]).then_inc(rec_dve, 1)

                    def normalise(done):
                        dve.wait_ge(spread_mm, done)
                        dve.wait_ge(oa_read, done)
                        nc.vector.tensor_tensor(weighed[:, :], weighed[:, :], mi[0:D, :], ALU.mult).then_inc(norm_dve, 1)

                    height_copy(H * NB)

                    def value_lo(u):
                        dve.wait_ge(prep_act, H * PREP_ACT + 8 + u + 1)
                        nc.vector.tensor_tensor(v_part(u, 1), v_tiles(u), v_part(u, 0), ALU.subtract).then_inc(prep_dve, 1)

                    column_max(H * NB, range(QT * NCH))
                    less_max(H * NB)
                    value_lo(24)
                    value_lo(25)
                    r_lo(H * NB, 0)
                    value_lo(26)
                    value_lo(27)

                    def body(ii, sl, before, after):
                        i = 2 * ii + sl
                        B = H * NB + i
                        for g in range(NG):
                            if before and g == TAKE_AT:
                                take_weighed(B)
                            if after and g == HEIGHT_COPY_AT:
                                height_copy(B + 1)
                            if after:
                                column_max(B + 1, MAX_AT[g])
                            if after and g == R_LO_AT:
                                r_lo(B + 1, 1 - sl)
                            if g >= 1:
                                low_probs(B, g - 1)
                            elif before:
                                low_probs(B - 1, NG - 1)
                            if after and g == LESS_AT:
                                less_max(B + 1)
                            if before and g == 3:
                                invert_totals(B)
                            if before and g == 5:
                                normalise(B)
                        if not after:
                            low_probs(B, NG - 1)
                            take_weighed(B + 1)
                            invert_totals(B + 1)
                            normalise(B + 1)

                    main_blocks(dve, body)

        @block.tensor
        def _(pe):
            pe.wait_ge(const_in, 16 * N_CONST)
            pe.wait_ge(hot_in, 32)
            pe.wait_ge(ones_set, 2)
            with pe.Fori(0, BATCH) as b:
                gn_scale(nc, "tensor", pe, b * GN_DVE, b, s, t)
                pe.wait_ge(s["gn_dve"], b * GN_DVE + GN_DVE)
                stand_apart(pe, passed)
                with pe.Fori(0, HEADS) as h:
                    H = b * HEADS + h
                    pe.wait_ge(wh_in, H * 80 + 80)
                    pe.wait_ge(exp_act, exp_count(H * NB, -1, 2))

                    def bank_free(u):
                        if 4 <= u < 12:
                            pe.wait_ge(prep_act, H * PREP_ACT + 2 * (u - 4) + 2)
                        if 4 <= u < 20:
                            pe.wait_ge(prep_dve, H * PREP_DVE + u - 4 + 1)
                        if u >= 20:
                            pe.wait_ge(prep_act, H * PREP_ACT + 8 + u - 4 + 1)

                    for u in range(NCH):
                        bank_free(u)
                        for k in range(KT):
                            mm = nc.tensor.matmul(unit_bank(u), w_head[:, k, :, :].rearrange("p a d -> p (a d)"),
                                                  xn[:, k, u * 512:(u + 1) * 512], start=(k == 0), stop=(k == KT - 1))
                        mm.then_inc(proj_mm, 1)
                    pe.wait_ge(prep_act, H * PREP_ACT + 16)
                    for u in range(8, 16):
                        bank_free(u)
                        stand_apart(pe, passed)
                        for j in range(8):
                            xq = (u - 8) * 8 + j
                            mm = nc.tensor.matmul(unit_bank(u)[D:P, j * HH:(j + 1) * HH], wrel[:, WW - 1 - xq:2 * WW - 1 - xq],
                                                  q_all[:, :].rearrange("p (y x) -> p x y", x=WW)[:, xq, :], start=True, stop=True)
                        mm.then_inc(proj_mm, 1)

                    def value_product(u, half, k):
                        first = half * 256
                        tokens = slice((u - 16) * 512 + first, (u - 16) * 512 + first + 256)
                        mm = nc.tensor.matmul(unit_bank(u)[0:D, first:first + 256], w_val[:, k, :], xn[:, k, tokens],
                                              start=(k == 0), stop=(k == KT - 1))
                        if half == 1 and k == KT - 1:
                            mm.then_inc(proj_mm, 1)

                    def turn_values(u):
                        bank_free(u)
                        stand_apart(pe, passed)
                        for j in range(4):
                            tile = slice(j * P, (j + 1) * P)
                            mm = nc.tensor.transpose(unit_bank(u)[:, tile], v_stage(u - 24)[:, tile], ident[:, :])
                        mm.then_inc(proj_mm, 1)

                    def height_logits(B, i):
                        pe.wait_ge(first_act, 3 * B + 1)
                        pe.wait_ge(lo_dve, B)
                        for qt in range(QT):
                            win = hrel[:, bass.ds(WW - 2 - 2 * qt - i * YQ, HH + 1)]
                            mm = nc.tensor.matmul(rh_ps[:, qt, 0:HH + 1], q_blk[:, qt * P:(qt + 1) * P], win, start=True, stop=True)
                        mm.then_inc(rh_mm, 1)

                    def max_scores(B, sl, k):
                        qt, c = divmod(k, NCH)
                        if k == 0:
                            pe.wait_ge(first_act, 3 * B + 3)
                            pe.wait_ge(rh_dve, B + 1)
                        elif k >= 2:
                            pe.wait_ge(mx_red, B * (QT * NCH) + k - 1)
                        nc.tensor.matmul(mx[:, k % 2, :], m_hi[:, sl, qt * P:(qt + 1) * P], k_pos[:, c * 512:(c + 1) * 512],
                                         start=True, stop=True).then_inc(mx_mm, 1)

                    def turn(B):
                        pe.wait_ge(rp_dve, 4 * B + 4)
                        for half in range(2):
                            for qt in range(QT):
                                mm = nc.tensor.transpose(mx[:, half, qt * P:(qt + 1) * P], r_less[:, qt, half * D:half * D + P], ident[:, :])
                        mm.then_inc(tr_mm, 1)

                    def scores(B, g, j, sl):
                        kt = g * GK + j
                        keys = slice(kt * P, (kt + 1) * P)
                        half, kp = divmod(kt, NKT // 2)
                        if j == 0:
                            pe.wait_ge(exp_act, exp_count(B, g - 2, 2))
                        nc.tensor.matmul(sc[:, g % 2, j, :], k_pos[:, keys], m_hi[:, sl, :], start=True, stop=False)
                        nc.tensor.matmul(sc[:, g % 2, j, :], k_hl[:, keys], m_lo[:, sl, :], start=False, stop=False)
                        mm = nc.tensor.matmul(sc[:, g % 2, j, :], pos[:, kp * P:(kp + 1) * P], m_pos[:, sl, half, :],
                                              start=False, stop=True)
                        if j == GK - 1:
                            mm.then_inc(score_mm, 1)

                    def weigh(B, g, part):
                        if part == 0:
                            pe.wait_ge(exp_act, exp_count(B, g, 2))
                            if g == 0:
                                pe.wait_ge(oa_read, B)
                        else:
                            pe.wait_ge(lo_p, LO0 + B * NG + g + 1)
                        for j in range(GK):
                            kt = g * GK + j
                            mm = nc.tensor.matmul(oa[:, :], v_hl[:, kt, :], (p_hi, p_lo)[part][:, g % 4, j, :],
                                                  start=(kt == 0 and part == 0), stop=(kt == NKT - 1 and part == 1))
                        if part == 1:
                            mm.then_inc(pv_mm, 1)

                    def totals(done, sl):
                        pe.wait_ge(sum_pool, SUM0 + done * NG)
                        pe.wait_ge(norm_dve, done - 1)
                        for qt in range(QT):
                            for j in range(GK):
                                mm = nc.tensor.matmul(mi[:, qt:qt + 1], p_sum[:, sl, j, qt * P:(qt + 1) * P], ones[:, 0:1],
                                                      start=(j == 0), stop=(j == GK - 1))
                        mm.then_inc(total_mm, 1)

                    def spread(done):
                        pe.wait_ge(rec_dve, done)
                        for qt in range(QT):
                            mm = nc.tensor.matmul(mi[0:D, qt * P:(qt + 1) * P], rec[:, qt:qt + 1].to_broadcast([P, D]), ident[:, :],
                                                  start=True, stop=True)
                        mm.then_inc(spread_mm, 1)

                    height_logits(H * NB, 0)
                    pe.wait_ge(prep_pool, H * NCH + NCH)
                    for u in range(16, 24):
                        bank_free(u)
                        for half in range(2):
                            for k in range(KT):
                                max_scores(H * NB, 0, 4 * (u - 16) + 2 * half + k)
                                value_product(u, half, k)
                    turn_values(24)
                    turn_values(25)
                    turn(H * NB)
                    turn_values(26)
                    turn_values(27)

                    def body(ii, sl, before, after):
                        i = 2 * ii + sl
                        B = H * NB + i

                        pe.wait_ge(lo_dve, B + 1)
                        pe.wait_ge(blk_act, B * BLK_ACT + BLK_ACT)
                        pe.wait_ge(blk_pool, B + 1)
                        stand_apart(pe, passed)
                        for g in range(NG):
                            ks = list(MAX_AT[g]) if after else []

                            def one_max():
                                if ks:
                                    max_scores(B + 1, 1 - sl, ks.pop(0))

                            if not before and g == 1:
                                pe.wait_ge(prep_dve, H * PREP_DVE + PREP_DVE)
                                stand_apart(pe, passed)
                            back = [(B, g - 3)] if g >= 3 else [(B - 1, n) for n in LAST_WEIGHED[g]] if before else []
                            scores(B, g, 0, sl)
                            one_max()
                            scores(B, g, 1, sl)
                            if after and g == HEIGHT_AT:
                                height_logits(B + 1, i + 1)
                            for part in range(2):
                                for group in back:
                                    weigh(*group, part)
                                one_max()
                            one_max()
                            if before and g == 2:
                                totals(B, 1 - sl)
                            if before and g == 4:
                                spread(B)
                            if after and g == TURN_AT:
                                turn(B + 1)
                        if not after:
                            for g in (NG - 3, NG - 2, NG - 1):
                                weigh(B, g, 0)
                                weigh(B, g, 1)
                            totals(B + 1, sl)
                            spread(B + 1)

                    main_blocks(pe, body)


def mamba_layer(nc, x1, out, w_to, b_to, w_in, conv_w, conv_b, w_x, w_dt, b_dt, a_log, d_skip, w_out, w_from, b_from,
                identity, group_mean, pick):
    with ExitStack() as ctx:
        def sb(name, shape, dt=F32):
            return ctx.enter_context(nc.sbuf_tensor(name, shape, dt))

        def sem(name):
            return ctx.enter_context(nc.semaphore(name))

        x_in_t = sb("m_x_in", [P, KT, T])
        x_res = sb("m_x_res", [P, KT, T])
        seq = sb("m_seq", [P, KT, T])
        u_raw = sb("m_u_raw", [P, DB, DC - 1 + T])
        u_conv = sb("m_u_conv", [P, DB, T])
        u_act = sb("m_u_act", [P, 2, DB, T])
        z_act = sb("m_z_act", [P, 2, DB, T])
        delta = sb("m_delta", [P, 2, DB, T])
        du = sb("m_du", [P, 2, DB, T])
        y = sb("m_y", [P, DB, T])
        bc = sb("m_bc", [2 * 2 * NS, 2, T], F32R)
        dt_low = sb("m_dt_low", [5 * NS, T])
        bc_all = sb("m_bc_all", [P, 2, 2, T])
        d_a = sb("m_d_a", [P, 2, DB, T])
        RING = 4
        ring = sb("m_ring", [P, RING, DB, T])
        state = sb("m_state", [P, DB, NS])
        o_in = sb("m_o_in", [P, KT, T])
        s_to, s_in = sb("m_w_to", [P, KT, C]), sb("m_w_in", [P, KT, 2 * DI])
        s_x, s_dt = sb("m_w_x", [P, DB, 5 * NS]), sb("m_w_dt", [5 * NS, DI])
        s_out, s_from = sb("m_w_out", [P, DB, C]), sb("m_w_from", [P, KT, C])
        s_bto, s_bfrom = sb("m_b_to", [P, KT]), sb("m_b_from", [P, KT])
        s_cw, s_cb, s_bdt, s_d = sb("m_conv_w", [P, DB, DC]), sb("m_conv_b", [P, DB]), sb("m_b_dt", [P, DB]), sb("m_d", [P, DB])
        a_exp, a_neg = sb("m_a_exp", [P, DB, NS]), sb("m_a_neg", [P, DB, NS])
        ident, gavg = sb("m_ident", [P, P]), sb("m_gavg", [P, P])
        s_pick = sb("m_pick", [2 * 2 * NS, 2 * NS, P], F32R)
        tiles = [gn_tiles(sb, f"m{b}") for b in range(BATCH)]
        log_e, low_e = y, u_conv
        xn_all = ring[:, :, :, :].rearrange("p r k t -> p (r k t)").rearrange("p (k l) -> p k l", k=KT)

        yp = ctx.enter_context(nc.psum_tensor("m_yp", [P, DB, T], F32))
        wk = ctx.enter_context(nc.psum_tensor("m_wk", [P, 4, T], F32))

        s = {n: sem("m_" + n) for n in ("gn_dve", "gn_pe", "gn_act")}
        passed = sem("m_passed")
        GN_BASE = [b * (GN_STATS + GN_SCALE) for b in range(BATCH)]
        for t in tiles:
            t["gavg"], t["gps"], t["passed"] = gavg, yp[:, 0, :], passed
        const_in, hot_in, all_in, xc_in, res_in, out_out = (
            sem("m_" + n) for n in ("const_in", "hot_in", "all_in", "xc_in", "res_in", "out_out"))
        wk_mm, wk_act, wk_dve = sem("m_wk_mm"), sem("m_wk_act"), sem("m_wk_dve")
        x_norm, halo, conv, act_u, act_z, dt_act = (sem("m_" + n) for n in ("x_norm", "halo", "conv", "act_u", "act_z", "dt_act"))
        v_act, e_act, log_act, one_dve, low_pool, sum_dve, delta_dve, du_dve = (
            sem("m_" + n) for n in ("v_act", "e_act", "log_act", "one_dve", "low_pool", "sum_dve", "delta_dve", "du_dve"))
        a_act, a_dve, state0 = sem("m_a_act"), sem("m_a_dve"), sem("m_state0")
        da_act, dbu, scan, st_dve, hc_done, y_mm, yd_dve, y_pool = (
            sem("m_" + n) for n in ("da_act", "dbu", "scan", "st_dve", "hc_done", "y_mm", "yd_dve", "y_pool"))
        NCHUNK = BATCH * NC

        FRONT = {1: ["SEQ0", "SEQ1"], 3: ["U0"], 4: ["U1"], 5: ["U2", "U3"], 6: ["Z0", "Z1"], 7: ["Z2"], 8: ["Z3"], 9: ["XD"],
                 10: ["DT0", "DT1"], 11: ["DT2", "DT3"]}
        CONV_AT, SILU_AT, BC_AT, EXP_AT, LOG_AT = 4, 8, 9, 12, 13
        SUM_AT, DELTA_AT, DU_AT = 13, 14, 14
        POST = {2: ["OUT0"], 3: ["OUT1"], 4: ["FROM0", "FROM1"]}

        def order(front, post, states, first_bc):
            units = []
            for n in range(NS):
                if states and n + 1 < NS + (1 if front else 0):
                    units += [f"B{(n + 1) % NS}", f"C{(n + 1) % NS}"]
                units += (FRONT.get(n, []) if front else []) + (POST.get(n, []) if post else [])
            return units + (["B0", "C0"] if first_bc else [])

        ORDER = {"pro": order(True, False, False, True), "first": order(True, False, True, False),
                 "mid": order(True, True, True, False), "last": order(False, True, True, False),
                 "epi": order(False, True, False, False)}

        def scalar_holds(name):
            return name[:2] != "SE" and name[:2] != "FR"

        def vector_holds(name):
            return name[:2] in ("SE", "FR", "XD")

        class BankCount:

            def __init__(self, kind, CH):
                self.kind, self.CH = kind, CH

            def before(self, counted):
                def n(kind):
                    return sum(counted(x) for x in ORDER[kind])
                if self.kind == "pro":
                    return 0
                if self.kind == "first":
                    return n("pro")
                if self.kind == "epi":
                    return n("pro") + n("first") + (NCHUNK - 2) * n("mid") + n("last")
                return n("pro") + n("first") + (self.CH - 1) * n("mid")

            def upto(self, name, counted):
                units = ORDER[self.kind]
                return self.before(counted) + sum(counted(x) for x in units[:units.index(name) + 1])

            def mm(self, name):
                return self.upto(name, lambda x: True)

            def act(self, name):
                return self.upto(name, scalar_holds)

            def dve(self, name):
                return self.upto(name, vector_holds)

            def bank(self, name):
                return wk[:, ORDER[self.kind].index(name) % 4, :]

        def at_least(e, sem_, value):
            if isinstance(value, int) and value <= 0:
                return
            e.wait_ge(sem_, value)

        def chunks(e, body):
            last = NC // 2 - 1
            for b in range(BATCH):
                for q in range(2):
                    body("first" if b == 0 and q == 0 else "mid", b, q, b * NC + q, q)
                with e.Fori(1, last) as cc:
                    for q in range(2):
                        body("mid", b, 2 * cc + q, 2 * cc + (b * NC + q), q)
                for q in range(2):
                    c = 2 * last + q
                    body("last" if b == BATCH - 1 and q == 1 else "mid", b, c, b * NC + c, q)

        def chunk_of(tensor, b, c, off):
            if isinstance(c, int):
                b, c = divmod(b * NC + c + off, NC)
                return tensor[b, :, c * T:(c + 1) * T].rearrange("(k p) l -> p k l", p=P)
            return tensor[b, :, bass.ds((c + off) * T, T)].rearrange("(k p) l -> p k l", p=P)

        block = ctx.enter_context(nc.Block())

        consts = [(s_to, w_to), (s_in, w_in), (s_x, w_x), (s_out, w_out), (s_from, w_from), (s_bto, b_to), (s_bfrom, b_from),
                  (s_cw, conv_w), (s_cb, conv_b), (s_bdt, b_dt), (s_d, d_skip), (a_exp, a_log), (ident, identity), (gavg, group_mean)]

        @block.sync
        def _(sp):
            sp.dma_start(xn_all, x1[0, :, :].rearrange("(k p) l -> p k l", p=P)).then_inc(all_in, 16)
            for dst, src in consts:
                sp.dma_start(dst[tuple(slice(None) for _ in dst.shape)], src).then_inc(const_in, 16)
            sp.dma_start(s_dt[4 * NS:5 * NS, :], w_dt).then_inc(const_in, 16)
            sp.dma_start(x_in_t[:, :, :], chunk_of(x1, 0, 0, 0)).then_inc(xc_in, 16)
            sp.dma_start(x_res[:, :, :], chunk_of(x1, 0, 0, 0)).then_inc(res_in, 16)
            for b in range(1, BATCH):
                sp.wait_ge(s["gn_dve"], GN_BASE[b - 1] + GN_STATS)
                sp.dma_start(xn_all, x1[b, :, :].rearrange("(k p) l -> p k l", p=P)).then_inc(all_in, 16)
            sp.wait_ge(wk_mm, BankCount("pro", 0).mm("SEQ1"))
            sp.dma_start(x_in_t[:, :, :], chunk_of(x1, 0, 0, 1)).then_inc(xc_in, 16)

            def body(kind, b, c, CH, q):
                at = BankCount(kind, CH)
                if kind != "last" and not (isinstance(CH, int) and CH + 2 >= NCHUNK):
                    sp.wait_ge(wk_mm, at.mm("SEQ1"))
                    sp.dma_start(x_in_t[:, :, :], chunk_of(x1, b, c, 2)).then_inc(xc_in, 16)
                if kind != "first":
                    sp.wait_ge(wk_dve, at.dve("FROM1"))
                    sp.dma_start(chunk_of(out, b, c, -1), x_res[:, :, :]).then_inc(out_out, 16)
                    sp.wait_ge(out_out, CH * 16)
                    sp.dma_start(x_res[:, :, :], chunk_of(x1, b, c, 0)).then_inc(res_in, 16)

            chunks(sp, body)
            sp.wait_ge(wk_dve, BankCount("epi", NCHUNK).dve("FROM1"))
            sp.dma_start(chunk_of(out, BATCH - 1, NC - 1, 0), x_res[:, :, :]).then_inc(out_out, 16)
            sp.wait_ge(out_out, 16 * NCHUNK)

        @block.gpsimd
        def _(pool):
            pool.dma_start(s_pick[:, :, :], pick).then_inc(hot_in, 16)

            def low_part(CH, q):
                pool.wait_ge(one_dve, CH + 1)
                nc.gpsimd.tensor_tensor(low_e[:, :, :], low_e[:, :, :], du[:, q, :, :], ALU.subtract).then_inc(low_pool, 1)

            def gate(CH, q):
                pool.wait_ge(yd_dve, (CH + 1) * DB)
                nc.gpsimd.tensor_tensor(y[:, :, :], y[:, :, :], z_act[:, q, :, :], ALU.mult).then_inc(y_pool, 1)

            low_part(0, 0)

            def body(kind, b, c, CH, q):
                at = BankCount(kind, CH)
                pool.wait_ge(du_dve, CH + 1)
                for n in range(NS):
                    if n == 0:
                        b_ready = BankCount("pro", 0).act("B0") if kind == "first" else at.before(scalar_holds) - 1
                    else:
                        b_ready = at.act(f"B{n}")
                    pool.wait_ge(wk_act, b_ready)
                    at_least(pool, y_mm, CH * NS + n - (RING - 1))
                    nc.gpsimd.tensor_tensor(ring[:, n % RING, :, :], du[:, q, :, :],
                                            bc_all[:, n % 2, 0:1, :].to_broadcast([P, DB, T]), ALU.mult).then_inc(dbu, 1)
                    if n == 1 and kind != "first":
                        gate(CH - 1, 1 - q)
                    if n == LOG_AT and kind != "last":
                        low_part(CH + 1, 1 - q)

            chunks(pool, body)
            gate(NCHUNK - 1, 1)

        @block.scalar
        def _(act):
            act.wait_ge(const_in, 16 * (len(consts) + 1))
            nc.scalar.activation(a_exp[:, :, :], a_exp[:, :, :], ACT.Exp).then_inc(a_act, 1)
            gn_scale(nc, "scalar", act, GN_BASE[0], 0, s, tiles[0])

            def front(at, n, CH, q):
                for name in FRONT.get(n, []):
                    k = int(name[-1]) if name != "XD" else 0
                    if name[0] == "U":
                        if k == 0:
                            act.wait_ge(halo, CH + 1)
                        act.wait_ge(wk_mm, at.mm(name))
                        nc.scalar.activation(u_raw[:, k, DC - 1:], at.bank(name), ACT.Copy).then_inc(wk_act, 1)
                    if name[0] == "Z":
                        act.wait_ge(wk_mm, at.mm(name))
                        at_least(act, y_pool, CH - 1)
                        nc.scalar.activation(z_act[:, q, k, :], at.bank(name), ACT.Copy).then_inc(wk_act, 1)
                    if name == "XD":
                        act.wait_ge(wk_mm, at.mm(name))
                        nc.scalar.activation(dt_low[4 * NS:5 * NS, :], at.bank(name)[4 * NS:5 * NS, :], ACT.Copy).then_inc(dt_act, 1)
                        nc.scalar.activation(bc[:, q, :], at.bank(name)[0:4 * NS, :], ACT.Copy).then_inc(wk_act, 1)
                    if name[0] == "D":
                        act.wait_ge(wk_mm, at.mm(name))
                        if k == 0:
                            at_least(act, dbu, (CH - 1) * NS)
                        nc.scalar.activation(delta[:, q, k, :], at.bank(name), ACT.Relu, bias=s_bdt[:, k:k + 1]).then_inc(v_act, 1)
                        nc.scalar.activation(du[:, q, k, :], at.bank(name), ACT.Abs, bias=s_bdt[:, k:k + 1]).then_inc(wk_act, 1)
                if n == SILU_AT:
                    act.wait_ge(conv, (CH + 1) * (DB * DC))
                    nc.scalar.activation(u_act[:, q, :, :], u_conv[:, :, :], ACT.Silu).then_inc(act_u, 1)
                    act.wait_ge(wk_act, at.act("Z3"))
                    nc.scalar.activation(z_act[:, q, :, :], z_act[:, q, :, :], ACT.Silu).then_inc(act_z, 1)
                if n == EXP_AT:
                    act.wait_ge(wk_act, at.act("DT3"))
                    nc.scalar.activation(du[:, q, :, :], du[:, q, :, :], ACT.Exp, scale=-1.0).then_inc(e_act, 1)
                if n == LOG_AT:
                    act.wait_ge(e_act, CH + 1)
                    nc.scalar.activation(log_e[:, :, :], du[:, q, :, :], ACT.Ln, bias=1.0).then_inc(log_act, 1)

            def copy_row(at, n, k, CH):
                name = f"{'BC'[k]}{n % NS}"
                act.wait_ge(wk_mm, at.mm(name))
                at_least(act, (dbu, hc_done)[k], CH * NS + n - 1)
                nc.scalar.activation(bc_all[:, n % 2, k, :], at.bank(name), ACT.Copy).then_inc(wk_act, 1)

            pro = BankCount("pro", 0)
            for n in range(NS):
                front(pro, n, 0, 0)
            for b in range(1, BATCH):
                gn_scale(nc, "scalar", act, GN_BASE[b], b, s, tiles[b])
            for k in range(2):
                copy_row(pro, 0, k, 0)

            def body(kind, b, c, CH, q):
                at = BankCount(kind, CH)
                act.wait_ge(delta_dve, CH + 1)
                act.wait_ge(a_dve, 1)
                for n in range(NS):
                    at_least(act, scan, CH * (NS * DB) + (n - 1) * DB)
                    for k in range(DB):
                        nc.scalar.activation(d_a[:, n % 2, k, :], delta[:, q, k, :], ACT.Exp, scale=a_neg[:, k, n:n + 1]).then_inc(da_act, 1)
                    if n + 1 < NS or kind != "last":
                        for k in range(2):
                            copy_row(at, n + 1, k, CH)
                    if kind != "last":
                        front(at, n, CH + 1, 1 - q)
                    if kind != "first":
                        post(at, n)

            def post(at, n):
                for name in POST.get(n, []):
                    if name[0] == "O":
                        act.wait_ge(wk_mm, at.mm(name))
                        nc.scalar.activation(o_in[:, int(name[-1]), :], at.bank(name), ACT.Copy).then_inc(wk_act, 1)

            chunks(act, body)
            for n in sorted(POST):
                post(BankCount("epi", NCHUNK), n)

        @block.vector
        def _(dve):
            dve.wait_ge(a_act, 1)
            nc.vector.tensor_scalar(a_neg[:, :, :], a_exp[:, :, :], -1.0, None, ALU.mult).then_inc(a_dve, 1)
            dve.wait_ge(all_in, 16)
            gn_stats(nc, dve, GN_BASE[0], xn_all, s, tiles[0])
            gn_scale(nc, "vector", dve, GN_BASE[0], 0, s, tiles[0])
            nc.vector.memset(state[:, :, :], 0.0).then_inc(state0, 1)
            nc.vector.memset(u_raw[:, :, 0:DC - 1], 0.0).then_inc(halo, 1)

            def front(at, n, CH, q, b):
                if n == 0:
                    dve.wait_ge(xc_in, 16 * CH + 16)
                    for k in range(KT):
                        nc.vector.tensor_scalar(x_in_t[:, k, :], x_in_t[:, k, :], tiles[b]["mg"][:, k, 0:1], tiles[b]["rs"][:, k:k + 1],
                                                ALU.subtract, ALU.mult).then_inc(x_norm, 1)
                if n == 1:
                    for k in range(KT):
                        dve.wait_ge(wk_mm, at.mm(f"SEQ{k}"))
                        nc.vector.tensor_scalar(seq[:, k, :], at.bank(f"SEQ{k}"), s_bto[:, k:k + 1], None, ALU.add).then_inc(wk_dve, 1)
                if CONV_AT <= n < CONV_AT + DB:
                    k = n - CONV_AT
                    dve.wait_ge(wk_act, at.act(f"U{k}"))
                    for tap in range(DC):
                        src = u_raw[:, k, tap:tap + T]
                        if tap == 0:
                            nc.vector.tensor_scalar(u_conv[:, k, :], src, s_cw[:, k, 0:1], s_cb[:, k:k + 1],
                                                    ALU.mult, ALU.add).then_inc(conv, 1)
                        else:
                            dve.wait_ge(conv, CH * (DB * DC) + k * DC + tap)
                            nc.vector.scalar_tensor_tensor(out=u_conv[:, k, :], in0=src, scalar=s_cw[:, k, tap:tap + 1],
                                                           in1=u_conv[:, k, :], op0=ALU.mult, op1=ALU.add).then_inc(conv, 1)
                    if k == DB - 1:
                        if isinstance(CH, int) and (CH + 1) % NC == 0:
                            nc.vector.memset(u_raw[:, :, 0:DC - 1], 0.0).then_inc(halo, 1)
                        else:
                            nc.vector.tensor_copy(u_raw[:, :, 0:DC - 1], u_raw[:, :, T:T + DC - 1]).then_inc(halo, 1)
                if n == BC_AT:
                    dve.wait_ge(wk_act, at.act("XD"))
                    nc.vector.tensor_tensor(bc[2 * NS:4 * NS, q, :], at.bank("XD")[2 * NS:4 * NS, :], bc[2 * NS:4 * NS, q, :],
                                            ALU.subtract).then_inc(wk_dve, 1)
                if n == EXP_AT:
                    dve.wait_ge(e_act, CH + 1)
                    dve.wait_ge(act_u, CH + 1)
                    nc.vector.tensor_scalar(low_e[:, :, :], du[:, q, :, :], 1.0, -1.0, ALU.add, ALU.add).then_inc(one_dve, 1)
                if n == SUM_AT:
                    dve.wait_ge(log_act, CH + 1)
                    dve.wait_ge(low_pool, CH + 1)
                    nc.vector.tensor_tensor(log_e[:, :, :], log_e[:, :, :], low_e[:, :, :], ALU.subtract).then_inc(sum_dve, 1)
                if n == DELTA_AT:
                    dve.wait_ge(sum_dve, CH + 1)
                    dve.wait_ge(v_act, (CH + 1) * DB)
                    nc.vector.tensor_tensor(delta[:, q, :, :], delta[:, q, :, :], log_e[:, :, :], ALU.add).then_inc(delta_dve, 1)
                if n == DU_AT:
                    dve.wait_ge(delta_dve, CH + 1)
                    nc.vector.tensor_tensor(du[:, q, :, :], delta[:, q, :, :], u_act[:, q, :, :], ALU.mult).then_inc(du_dve, 1)

            def skip(CH, q):
                dve.wait_ge(y_mm, (CH + 1) * NS)
                for k in range(DB):
                    nc.vector.scalar_tensor_tensor(out=y[:, k, :], in0=u_act[:, q, k, :], scalar=s_d[:, k:k + 1],
                                                   in1=yp[:, k, :], op0=ALU.mult, op1=ALU.add).then_inc(yd_dve, 1)

            def residual(at, CH):
                dve.wait_ge(res_in, 16 * CH + 16)
                for k in range(KT):
                    dve.wait_ge(wk_mm, at.mm(f"FROM{k}"))
                    nc.vector.scalar_tensor_tensor(out=x_res[:, k, :], in0=at.bank(f"FROM{k}"), scalar=s_bfrom[:, k:k + 1],
                                                   in1=x_res[:, k, :], op0=ALU.add, op1=ALU.add).then_inc(wk_dve, 1)

            for n in range(NS):
                front(BankCount("pro", 0), n, 0, 0, 0)
                if n == BC_AT:
                    for b in range(1, BATCH):
                        dve.wait_ge(all_in, 16 * b + 16)
                        gn_stats(nc, dve, GN_BASE[b], xn_all, s, tiles[b])
            for b in range(1, BATCH):
                gn_scale(nc, "vector", dve, GN_BASE[b], b, s, tiles[b])

            def body(kind, b, c, CH, q):
                at = BankCount(kind, CH)
                if isinstance(CH, int) and CH % NC == 0 and CH > 0:
                    dve.wait_ge(st_dve, CH * NS)
                    nc.vector.memset(state[:, :, :], 0.0).then_inc(state0, 1)
                for n in range(NS):
                    r = n % RING
                    dve.wait_ge(dbu, CH * NS + n + 1)
                    if n == 0:
                        at_least(dve, st_dve, CH * NS)
                        dve.wait_ge(state0, b + 1)
                    for k in range(DB):
                        dve.wait_ge(da_act, CH * (NS * DB) + n * DB + k + 1)
                        nc.vector.tensor_tensor_scan(ring[:, r, k, :], d_a[:, n % 2, k, :], ring[:, r, k, :],
                                                     state[:, k, n:n + 1], ALU.mult, ALU.add).then_inc(scan, 1)
                    dve.wait_ge(scan, CH * (NS * DB) + (n + 1) * DB)
                    nc.vector.tensor_copy(state[:, :, n], ring[:, r, :, T - 1]).then_inc(st_dve, 1)
                    if n == 0 and kind != "first":
                        skip(CH - 1, 1 - q)
                    if kind != "last":
                        front(at, n, CH + 1, 1 - q, (b + 1 if c == NC - 1 else b) if isinstance(c, int) else b)
                    dve.wait_ge(st_dve, CH * NS + n + 1)
                    if n == 0:
                        c_ready = BankCount("pro", 0).act("C0") if kind == "first" else at.before(scalar_holds)
                    else:
                        c_ready = at.act(f"C{n}")
                    dve.wait_ge(wk_act, c_ready)
                    nc.vector.tensor_tensor(ring[:, r, :, :], ring[:, r, :, :],
                                            bc_all[:, n % 2, 1:2, :].to_broadcast([P, DB, T]), ALU.mult).then_inc(hc_done, 1)
                    if n == max(POST) and kind != "first":
                        residual(at, CH - 1)

            chunks(dve, body)
            skip(NCHUNK - 1, 1)
            residual(BankCount("epi", NCHUNK), NCHUNK - 1)

        @block.tensor
        def _(pe):
            pe.wait_ge(const_in, 16 * (len(consts) + 1))
            pe.wait_ge(hot_in, 16)
            gn_scale(nc, "tensor", pe, GN_BASE[0], 0, s, tiles[0])

            def bank_free(at, name):
                units = ORDER[at.kind]
                i = units.index(name)
                if i < 4:
                    at_least(pe, wk_act, at.before(scalar_holds))
                    at_least(pe, wk_dve, at.before(vector_holds))
                elif vector_holds(units[i - 4]):
                    pe.wait_ge(wk_dve, at.dve(units[i - 4]))
                else:
                    pe.wait_ge(wk_act, at.act(units[i - 4]))

            def project(at, name, w, m, src, k_tiles):
                bank_free(at, name)
                for k in range(k_tiles):
                    mm = nc.tensor.matmul(at.bank(name), w[:, k, m * P:(m + 1) * P], src(k), start=(k == 0), stop=(k == k_tiles - 1))
                mm.then_inc(wk_mm, 1)

            def front(at, n, CH, q):
                for name in FRONT.get(n, []):
                    m = int(name[-1]) if name != "XD" else 0
                    if name == "SEQ0":
                        pe.wait_ge(x_norm, KT * CH + KT)
                    if name == "U0":
                        pe.wait_ge(wk_dve, at.dve("SEQ1"))
                    if name[0] == "S":
                        project(at, name, s_to, m, lambda k: x_in_t[:, k, :], KT)
                    if name[0] == "U":
                        project(at, name, s_in, m, lambda k: seq[:, k, :], KT)
                    if name[0] == "Z":
                        project(at, name, s_in, DB + m, lambda k: seq[:, k, :], KT)
                    if name == "XD":
                        pe.wait_ge(act_u, CH + 1)
                        bank_free(at, name)
                        for k in range(DB):
                            mm = nc.tensor.matmul(at.bank(name)[0:5 * NS, :], s_x[:, k, :], u_act[:, q, k, :], start=(k == 0), stop=(k == DB - 1))
                        mm.then_inc(wk_mm, 1)
                    if name[0] == "D":
                        if m == 0:
                            pe.wait_ge(dt_act, CH + 1)
                        bank_free(at, name)
                        nc.tensor.matmul(at.bank(name), s_dt[4 * NS:5 * NS, m * P:(m + 1) * P], dt_low[4 * NS:5 * NS, :],
                                         start=True, stop=True).then_inc(wk_mm, 1)

            def post(at, n, CH):
                for name in POST.get(n, []):
                    m = int(name[-1])
                    if name[0] == "O":
                        if m == 0:
                            pe.wait_ge(y_pool, CH + 1)
                        project(at, name, s_out, m, lambda k: y[:, k, :], DB)
                    else:
                        if m == 0:
                            pe.wait_ge(wk_act, at.act("OUT1"))
                        project(at, name, s_from, m, lambda k: o_in[:, k, :], KT)

            def copy_rows(at, n, q):
                for k in range(2):
                    name = f"{'BC'[k]}{n % NS}"
                    bank_free(at, name)
                    nc.tensor.matmul(at.bank(name), s_pick[:, k * NS + n % NS, :], bc[:, q, :], start=True, stop=True).then_inc(wk_mm, 1)

            pro = BankCount("pro", 0)
            for n in range(NS):
                front(pro, n, 0, 0)
            pe.wait_ge(wk_dve, pro.dve("XD"))
            copy_rows(pro, 0, 0)
            for b in range(1, BATCH):
                gn_scale(nc, "tensor", pe, GN_BASE[b], b, s, tiles[b])

            def body(kind, b, c, CH, q):
                at = BankCount(kind, CH)

                def add_up(n):
                    pe.wait_ge(hc_done, CH * NS + n + 1)
                    if n == 0:
                        at_least(pe, yd_dve, CH * DB)
                    for k in range(DB):
                        mm = nc.tensor.matmul(yp[:, k, :], ident[:, :], ring[:, n % RING, k, :], start=(n == 0), stop=(n == NS - 1))
                    mm.then_inc(y_mm, 1)

                for n in range(NS):
                    if n + 1 < NS:
                        copy_rows(at, n + 1, q)
                    elif kind != "last":
                        pe.wait_ge(wk_dve, at.dve("XD"))
                        copy_rows(at, n + 1, 1 - q)
                    if kind != "last":
                        front(at, n, CH + 1, 1 - q)
                    if kind != "first":
                        post(at, n, CH - 1)
                    if n >= 1:
                        add_up(n - 1)
                add_up(NS - 1)

            chunks(pe, body)
            for n in sorted(POST):
                post(BankCount("epi", NCHUNK), n, NCHUNK - 1)


ATT_IN = ["w_qk", "w_v", "height_rel", "width_rel", "key_hot", "pos_hot", "identity", "group_mean"]
MAM_IN = ["w_to", "b_to", "w_in", "conv_w", "conv_b", "w_x", "w_dt", "b_dt", "a_log", "d_skip", "w_out", "w_from", "b_from",
          "identity", "group_mean", "pick"]


def lay_out(inputs):
    import numpy as np

    a = {k: np.asarray(v) for k, v in inputs.items()}
    w = a["L0_conv_qkv_w"]
    key = np.arange(L)
    key_hot = (key[None, :] % WW == np.arange(WW)[:, None]).astype(np.float32)
    row_hot = (key[None, :L // 2] // WW == np.arange(HH // 2)[:, None]).astype(np.float32)
    channel = np.arange(P)

    def rows(v):
        return np.ascontiguousarray(np.swapaxes(v.reshape(v.shape[0] // P, P, *v.shape[1:]), 0, 1))

    w_x = a["L1_conv_x_proj_w"].T
    w_dt_cols, w_bc_cols = w_x[:, :DR], w_x[:, DR:]
    pick = np.zeros((2, 2 * NS, 2 * NS, P), np.float32)
    pick[:, np.arange(2 * NS), np.arange(2 * NS), :] = 1
    return {
        "x": a["x"].reshape(BATCH, C, L),
        "w_qk": np.ascontiguousarray(w[:2 * C].reshape(2, HEADS, D, C).transpose(3, 1, 0, 2)),
        "w_v": np.ascontiguousarray(w[2 * C:].T.reshape(KT, P, C).transpose(1, 0, 2)),
        "height_rel": np.ascontiguousarray(a["L0_conv_height_rel"].T),
        "width_rel": np.ascontiguousarray(a["L0_conv_width_rel"].T),
        "key_hot": key_hot,
        "pos_hot": np.concatenate([key_hot[:, :L // 2], row_hot, row_hot]),
        "identity": np.eye(P, dtype=np.float32),
        "group_mean": (channel[:, None] // 8 == channel[None, :] // 8).astype(np.float32) / 8,
        "w_to": rows(a["L1_conv_to_seq_w"].T),
        "b_to": rows(a["L1_conv_to_seq_b"]),
        "w_in": rows(a["L1_conv_in_proj_w"].T),
        "conv_w": rows(a["L1_conv_conv_w"]),
        "conv_b": rows(a["L1_conv_conv_b"]),
        "w_x": rows(np.concatenate([w_bc_cols, w_bc_cols, w_dt_cols], axis=1)),
        "w_dt": np.ascontiguousarray(a["L1_conv_dt_proj_w"].T),
        "b_dt": rows(a["L1_conv_dt_proj_b"]),
        "a_log": rows(a["L1_conv_A_log"]),
        "d_skip": rows(a["L1_conv_D"]),
        "w_out": rows(a["L1_conv_out_proj_w"].T),
        "w_from": rows(a["L1_conv_from_seq_w"].T),
        "b_from": rows(a["L1_conv_from_seq_b"]),
        "pick": pick.reshape(4 * NS, 2 * NS, P),
    }


def kernel(**inputs):
    import numpy as np
    from concourse import bacc
    from concourse.bass_utils import run_bass_kernel_spmd

    arrays = lay_out(inputs)
    nc = bacc.Bacc("TRN2", target_bir_lowering=False, num_devices=1)
    dram = {n: nc.dram_tensor(n, v.shape, mybir.dt.from_np(v.dtype), kind="ExternalInput").ap() for n, v in arrays.items()}
    x1 = nc.dram_tensor("x1", [BATCH, C, L], F32).ap()
    out = nc.dram_tensor("out", [BATCH, C, L], F32, kind="ExternalOutput").ap()
    attention_layer(nc, dram["x"], x1, *[dram[n] for n in ATT_IN])
    mamba_layer(nc, x1, out, *[dram[n] for n in MAM_IN])
    r = run_bass_kernel_spmd(nc, [arrays], core_ids=[0])
    return r.results[0]["out"].reshape(BATCH, C, HH, WW)
```
